# Optimizing a Trainium2 kernel written in Bass

```python
import numpy as np
import jax
import jax.numpy as jnp

def _softmax(x, axis=-1):
    return jax.nn.softmax(x, axis=axis)

def _gelu(x):
    return jax.nn.gelu(x, approximate=True)

def _silu(x):
    return jax.nn.silu(x)

def _sigmoid(x):
    return jax.nn.sigmoid(x)

def _layernorm(x, axis=-1, eps=1e-05):
    m = jnp.mean(x, axis=axis, keepdims=True)
    v = jnp.var(x, axis=axis, keepdims=True)
    return (x - m) / jnp.sqrt(v + eps)

def _scatter_add(tgt, idx, src, axis=0):
    return tgt.at[idx].add(src)

def _segment_sum(src, seg, n):
    return jax.ops.segment_sum(src, seg, n)
kernel_name = 'mk_decoder_preln_d1_seqx_r4_88b04d'

def setup_inputs(seed: int=0):
    np.random.seed(seed)
    _w = jnp.asarray

    def _rec_inputs():
        import jax
        import jax.numpy as jnp
        _rk = jax.random.key(seed)
        x = -0.0002928 + 1 * jax.random.normal(jax.random.fold_in(_rk, 1), (4, 512, 256), jnp.float32)
        _lenS = 512 - jax.random.randint(jax.random.fold_in(_rk, 7), (4,), 0, max(1, 512 // 4) + 1, jnp.int32)
        _lenS2 = 1601 - jax.random.randint(jax.random.fold_in(_rk, 8), (4,), 0, max(1, 1601 // 4) + 1, jnp.int32)
        _ctx_1024P = jax.random.normal(jax.random.fold_in(_rk, 11), (4, 16, 256), jnp.float32)
        _ctx_1024c = jax.random.dirichlet(jax.random.fold_in(_rk, 511), 0.3 * jnp.ones((16,), jnp.float32), (4, 1601))
        _ctx_1024t = jnp.einsum('bsk,bkd->bsd', _ctx_1024c, _ctx_1024P)
        _ctx_1024t = _ctx_1024t * jax.lax.rsqrt(jnp.mean(jnp.square(_ctx_1024t)) + 1e-12) * 0.953939
        ctx_1024 = -1.39393e-06 + 0.999914 * (_ctx_1024t + 0.3 * jax.random.normal(jax.random.fold_in(_rk, 611), (4, 1601, 256), jnp.float32))
        return (x, ctx_1024)
    x, ctx_1024 = _rec_inputs()

    def _L0_attn_setup():
        import jax, jax.numpy as jnp
        import numpy as np
        LN_EPS = 1e-05
        NUM_HEAD = 16
        key = jax.random.key(seed)
        ks = jax.random.split(key, 10)
        B, S, E = (2, 512, 256)
        sc = 0.02
        return {'x': jax.random.normal(ks[0], (B, S, E), jnp.float32), 'wq': jax.random.normal(ks[1], (E, E), jnp.float32) * sc, 'bq': jax.random.normal(ks[2], (E,), jnp.float32) * sc, 'wk': jax.random.normal(ks[3], (E, E), jnp.float32) * sc, 'bk': jax.random.normal(ks[4], (E,), jnp.float32) * sc, 'wv': jax.random.normal(ks[5], (E, E), jnp.float32) * sc, 'bv': jax.random.normal(ks[6], (E,), jnp.float32) * sc, 'wo': jax.random.normal(ks[7], (E, E), jnp.float32) * sc, 'bo': jax.random.normal(ks[8], (E,), jnp.float32) * sc, 'gamma': jnp.ones((E,), jnp.float32), 'beta': jnp.zeros((E,), jnp.float32)}
    _L0_attn_all = _L0_attn_setup()
    _L0_attn_in = {k: v for k, v in _L0_attn_all.items() if k in ('wq', 'bq', 'wk', 'bk', 'wv', 'bv', 'wo', 'bo', 'gamma', 'beta')}
    del _L0_attn_all

    def _L0_xattn_setup():
        import jax, jax.numpy as jnp
        import numpy as np
        D_MODEL = 256
        N_HEADS = 16
        D_HEAD = D_MODEL // N_HEADS
        key = jax.random.key(seed)
        ks = jax.random.split(key, 7)
        B, L = (2, 512)
        s = 1.0 / np.sqrt(D_MODEL)
        return {'q': jax.random.normal(ks[0], (B, L, D_MODEL), dtype=jnp.float32), 'k': jax.random.normal(ks[1], (B, L, D_MODEL), dtype=jnp.float32), 'v': jax.random.normal(ks[2], (B, L, D_MODEL), dtype=jnp.float32), 'Wq': jax.random.normal(ks[3], (D_MODEL, D_MODEL), dtype=jnp.float32) * s, 'Wk': jax.random.normal(ks[4], (D_MODEL, D_MODEL), dtype=jnp.float32) * s, 'Wv': jax.random.normal(ks[5], (D_MODEL, D_MODEL), dtype=jnp.float32) * s, 'Wo': jax.random.normal(ks[6], (D_MODEL, D_MODEL), dtype=jnp.float32) * s}
    _L0_xattn_all = _L0_xattn_setup()
    _L0_xattn_in = {k: v for k, v in _L0_xattn_all.items() if k in ('Wq', 'Wk', 'Wv', 'Wo')}
    del _L0_xattn_all

    def _L0_ffn_setup():
        import jax, jax.numpy as jnp
        import numpy as np
        D = 256
        H = 256
        E = 8
        K = 2
        I = 2 * 256
        ROUTE_SCALE = 1.0
        key = jax.random.key(seed)
        ks = jax.random.split(key, 12)
        s = lambda *sh: 1.0 / np.sqrt(sh[-1])
        return {'x': jax.random.normal(ks[0], (1, 512, D), jnp.float32), 'gate_w': jax.random.normal(ks[1], (E, D), jnp.float32) * s(E, D), 'w1': jax.random.normal(ks[2], (E, H, D), jnp.float32) * s(H, D), 'b1': jax.random.normal(ks[3], (E, H), jnp.float32) * 0.01, 'w2': jax.random.normal(ks[4], (E, D, H), jnp.float32) * s(D, H), 'b2': jax.random.normal(ks[5], (E, D), jnp.float32) * 0.01, 'w3': jax.random.normal(ks[6], (E, H, D), jnp.float32) * s(H, D), 'b3': jax.random.normal(ks[7], (E, H), jnp.float32) * 0.01, 'sw1': jax.random.normal(ks[8], (I, D), jnp.float32) * s(I, D), 'sw2': jax.random.normal(ks[9], (I, D), jnp.float32) * s(I, D), 'sw3': jax.random.normal(ks[10], (D, I), jnp.float32) * s(D, I)}
    _L0_ffn_all = _L0_ffn_setup()
    _L0_ffn_in = {k: v for k, v in _L0_ffn_all.items() if k in ('gate_w', 'w1', 'b1', 'w2', 'b2', 'w3', 'b3', 'sw1', 'sw2', 'sw3')}
    del _L0_ffn_all
    return {'x': x, 'ctx_1024': ctx_1024, 'L0_attn_wq': _L0_attn_in['wq'], 'L0_attn_bq': _L0_attn_in['bq'], 'L0_attn_wk': _L0_attn_in['wk'], 'L0_attn_bk': _L0_attn_in['bk'], 'L0_attn_wv': _L0_attn_in['wv'], 'L0_attn_bv': _L0_attn_in['bv'], 'L0_attn_wo': _L0_attn_in['wo'], 'L0_attn_bo': _L0_attn_in['bo'], 'L0_attn_gamma': _L0_attn_in['gamma'], 'L0_attn_beta': _L0_attn_in['beta'], 'L0_xattn_Wq': _L0_xattn_in['Wq'], 'L0_xattn_Wk': _L0_xattn_in['Wk'], 'L0_xattn_Wv': _L0_xattn_in['Wv'], 'L0_xattn_Wo': _L0_xattn_in['Wo'], 'L0_ffn_gate_w': _L0_ffn_in['gate_w'], 'L0_ffn_w1': _L0_ffn_in['w1'], 'L0_ffn_b1': _L0_ffn_in['b1'], 'L0_ffn_w2': _L0_ffn_in['w2'], 'L0_ffn_b2': _L0_ffn_in['b2'], 'L0_ffn_w3': _L0_ffn_in['w3'], 'L0_ffn_b3': _L0_ffn_in['b3'], 'L0_ffn_sw1': _L0_ffn_in['sw1'], 'L0_ffn_sw2': _L0_ffn_in['sw2'], 'L0_ffn_sw3': _L0_ffn_in['sw3']}

def reference(x, ctx_1024, L0_attn_wq, L0_attn_bq, L0_attn_wk, L0_attn_bk, L0_attn_wv, L0_attn_bv, L0_attn_wo, L0_attn_bo, L0_attn_gamma, L0_attn_beta, L0_xattn_Wq, L0_xattn_Wk, L0_xattn_Wv, L0_xattn_Wo, L0_ffn_gate_w, L0_ffn_w1, L0_ffn_b1, L0_ffn_w2, L0_ffn_b2, L0_ffn_w3, L0_ffn_b3, L0_ffn_sw1, L0_ffn_sw2, L0_ffn_sw3):
    import jax
    import jax.numpy as jnp

    def _L0_attn_ref(x, wq, bq, wk, bk, wv, bv, wo, bo, gamma, beta):
        import jax, jax.numpy as jnp
        import numpy as np
        LN_EPS = 1e-05
        NUM_HEAD = 16
        B, S, E = x.shape
        H = NUM_HEAD
        D = E // H
        Q = x @ wq + bq
        K = x @ wk + bk
        V = x @ wv + bv
        Q = Q.reshape(B * H, S, D)
        K = K.reshape(B * H, S, D)
        V = V.reshape(B * H, S, D)
        scores = jnp.einsum('bqd,bkd->bqk', Q, K) / jnp.sqrt(jnp.float32(D))
        attn = jax.nn.softmax(scores, axis=-1)
        ctx = jnp.einsum('bqk,bkd->bqd', attn, V)
        ctx = ctx.reshape(B, S, E)
        out = ctx @ wo + bo
        out = out + x
        mu = jnp.mean(out, axis=-1, keepdims=True)
        var = jnp.var(out, axis=-1, keepdims=True)
        out = (out - mu) * jax.lax.rsqrt(var + LN_EPS) * gamma + beta
        return out

    def _L0_xattn_ref(q, k, v, Wq, Wk, Wv, Wo):
        import jax, jax.numpy as jnp
        import numpy as np
        D_MODEL = 256
        N_HEADS = 16
        D_HEAD = D_MODEL // N_HEADS
        B, Lq, _ = q.shape
        Lk = k.shape[1]
        qh = (q @ Wq.T).reshape(B, Lq, N_HEADS, D_HEAD).transpose(0, 2, 1, 3)
        kh = (k @ Wk.T).reshape(B, Lk, N_HEADS, D_HEAD).transpose(0, 2, 1, 3)
        vh = (v @ Wv.T).reshape(B, Lk, N_HEADS, D_HEAD).transpose(0, 2, 1, 3)
        scores = jnp.einsum('bhqd,bhkd->bhqk', qh, kh) / jnp.sqrt(jnp.asarray(D_HEAD, dtype=qh.dtype))
        attn = jax.nn.softmax(scores, axis=-1)
        out = jnp.einsum('bhqk,bhkd->bhqd', attn, vh)
        out = out.transpose(0, 2, 1, 3).reshape(B, Lq, D_MODEL)
        return out @ Wo.T

    def _L0_ffn_ref(x, gate_w, w1, b1, w2, b2, w3, b3, sw1, sw2, sw3):
        import jax, jax.numpy as jnp
        import numpy as np
        D = 256
        H = 256
        E = 8
        K = 2
        I = 2 * 256
        ROUTE_SCALE = 1.0
        B, S, _ = x.shape
        xt = x.reshape(-1, D)
        logits = xt @ gate_w.T
        scores = jax.nn.softmax(logits.astype(jnp.float32), axis=-1)
        top_vals, idx = jax.lax.top_k(scores, K)
        weights = jnp.take_along_axis(scores, idx, axis=1).astype(x.dtype) * ROUTE_SCALE
        xs = xt[:, None, :] * weights[:, :, None]
        y = jnp.zeros_like(xt)
        for e in range(E):
            mask = (idx == e).astype(x.dtype)
            h = jax.nn.silu(jnp.einsum('tkd,hd->tkh', xs, w1[e]) + b1[e])
            x2 = jnp.einsum('tkh,dh->tkd', h, w2[e]) + b2[e]
            x3 = jnp.einsum('tkd,hd->tkh', xs, w3[e]) + b3[e]
            y = y + jnp.sum(x2 * x3 * mask[:, :, None], axis=1)
        z = jax.nn.silu(xt @ sw1.T) * (xt @ sw2.T) @ sw3.T
        return (y + z).reshape(B, S, D)
    x = x + _L0_attn_ref(_layernorm(x, axis=-1), L0_attn_wq, L0_attn_bq, L0_attn_wk, L0_attn_bk, L0_attn_wv, L0_attn_bv, L0_attn_wo, L0_attn_bo, L0_attn_gamma, L0_attn_beta)
    x = x + _L0_xattn_ref(_layernorm(x, axis=-1), ctx_1024, ctx_1024, L0_xattn_Wq, L0_xattn_Wk, L0_xattn_Wv, L0_xattn_Wo)
    x = x + _L0_ffn_ref(_layernorm(x, axis=-1), L0_ffn_gate_w, L0_ffn_w1, L0_ffn_b1, L0_ffn_w2, L0_ffn_b2, L0_ffn_w3, L0_ffn_b3, L0_ffn_sw1, L0_ffn_sw2, L0_ffn_sw3)
    return x

_drawn_inputs = setup_inputs


def setup_inputs(seed=0):
    import zlib

    import numpy as np

    out = dict(_drawn_inputs(seed))
    spreads = {'L0_attn_gamma': (1.0, 0.2), 'L0_attn_beta': (0.0, 0.1)}
    factors = {'L0_attn_wq': 8.0,
     'L0_attn_bq': 8.0,
     'L0_attn_wk': 8.0,
     'L0_attn_bk': 8.0,
     'L0_attn_wv': 8.0,
     'L0_attn_bv': 8.0,
     'L0_attn_wo': 8.0,
     'L0_attn_bo': 20.301,
     'L0_ffn_b1': 42.787,
     'L0_ffn_b2': 8.0,
     'L0_ffn_b3': 38.105}
    for name, (base, spread) in spreads.items():
        noise = np.random.default_rng([zlib.crc32(name.encode()), seed]).standard_normal(out[name].shape)
        drawn = base * np.exp(spread * noise) if base else spread * noise
        out[name] = jnp.asarray(drawn.astype(out[name].dtype))
    for name, factor in factors.items():
        out[name] = (out[name] * factor).astype(out[name].dtype)
    return out
```

```python
from contextlib import nullcontext

import numpy as np
import concourse.bass as bass
from concourse import mybir

F32 = mybir.dt.float32
BF16 = mybir.dt.bfloat16
I32 = mybir.dt.int32
U32 = mybir.dt.uint32
ACT = mybir.ActivationFunctionType
ALU = mybir.AluOpType
AX = mybir.AxisListType
ds = bass.ds

P = 128
B, S, D = 4, 512, 256
SK = 1601
HEADS, HD = 16, 16
TOK = B * S
TILES = TOK // P
KC = D // P
SKP = 1664
XT = (SK + P - 1) // P
XLAST = SK - (XT - 1) * P
KB = 401
KB0 = [0, KB, 2 * KB, SK - KB]
ST = S // P
GROUPS = 16
PARTS = 3
ROWS = 6 * HD
Q_PART = [0, 1, 2, 0, 1, 0]
K_PART = [0, 0, 0, 1, 1, 2]
EXPERTS, HID, INNER = 8, 256, 512
SLOT_TILES = 40
LN_EPS = 1e-5
SCALE = HD ** -0.5
DEN_LOW, DEN_HIGH = 1e-25, 1e34


class Arena:

    def __init__(self, tensor, words):
        self.t, self.words = tensor, words

    def at(self, off, shape, dt=F32):
        n = int(np.prod(shape))
        w = n if dt != BF16 else (n + 1) // 2
        assert off + w <= self.words, (off, w, self.words)
        v = self.t[:, off:off + w]
        if dt != F32:
            v = v.bitcast(dt)
        if dt == BF16 and 2 * w != n:
            v = v[:, 0:n]
        if len(shape) > 1:
            names = [f"a{i}" for i in range(len(shape))]
            v = v.rearrange(f"p ({' '.join(names)}) -> p {' '.join(names)}", **dict(zip(names, shape)))
        return v, off + w


def build(nc, x, ctxT, w_self, bqk, bv, bo, gamma, beta, w_cross, wo_cross, gate, w13, b13, w2, b2, sw12, sw3,
          ident_in, lower_in, before_in, steps_in, out):
    def dram(name, shape, dt):
        return nc.dram_tensor(name, shape, dt, kind="Internal").ap()

    qk_self = dram("qk_self", (B, 2, PARTS, D, S), BF16)
    q_cross = dram("q_cross", (GROUPS, PARTS, 64, S), BF16)
    k_cross = dram("k_cross", (GROUPS, PARTS, 64, SKP), BF16)
    m_self = dram("m_self", (B, HEADS, S), BF16)
    m_cross = dram("m_cross", (GROUPS, 4, S), BF16)

    x_slots = dram("x_slots", (SLOT_TILES * P, D), F32)
    y_slots = dram("y_slots", (SLOT_TILES * P, D), F32)

    WORDS = 52900
    arena = Arena(nc.alloc_sbuf_tensor("arena", [P, WORDS], F32), WORDS)
    xt, o = arena.at(0, (TILES, D))
    o_xn = o
    xn, o = arena.at(o, (TILES, D))
    xT, o = arena.at(o, (KC, TOK))
    ctxn = xT.rearrange("p c t -> p (c t)").rearrange("p (t d) -> p t d", d=D)
    cT, _ = arena.at(o_xn, (GROUPS, S))
    ident, o = arena.at(o, (P,))
    ones, o = arena.at(o, (P,))
    eps, o = arena.at(o, (1,))
    stats, o = arena.at(o, (TILES, 6))
    mv, o = arena.at(o, (TILES, 2))
    std, o = arena.at(o, (TILES,))
    rstd, o = arena.at(o, (TILES,))
    low, o = arena.at(o, (GROUPS,))
    high, o = arena.at(o, (GROUPS,))
    good, o = arena.at(o, (4,))
    flag, o = arena.at(o, (2,), I32)
    turned, o = arena.at(o, (2, S))
    recip, o = arena.at(o, (2, 16))
    normed, o = arena.at(o, (2, S))
    back, o = arena.at(o, (2, S))
    o_w = o
    wqk, o = arena.at(o_w, (3, KC, D))
    wo_s, o = arena.at(o, (KC, D))
    wx, o = arena.at(o, (3, KC, D))
    wox, _ = arena.at(o_w, (4, D))
    bqk_sb, o = arena.at(o, (2, KC))
    bo_bc, o = arena.at(o, (D,))
    ga_bc, o = arena.at(o, (D,))
    be_bc, o = arena.at(o, (D,))
    bv_row, o = arena.at(o, (D,))
    base = o
    vself, o = arena.at(base, (TILES, 4, ST, HD))
    qx_s, o = arena.at(o, (2, HEADS, S), BF16)
    kx_s, o = arena.at(o, (2, HEADS, S), BF16)
    kraw, o = arena.at(o, (HEADS, S), BF16)
    o_p = max(o, base + GROUPS * XT * 64 + 8448)
    vcross, o = arena.at(base, (GROUPS, XT, 64))
    o_kx = o
    kx_c, o = arena.at(o, (2, 4, SK + 1), BF16)
    qx_c, o = arena.at(o, (2, 4, S), BF16)
    ctx_sb, oc = arena.at(o_kx, (2, KC, SK))
    assert max(o, oc) <= o_p
    probs, o = arena.at(o_p, (2, 4, S))
    vg, o = arena.at(o, (2, XT, 4, 32))
    parts, _ = arena.at(o_p, (4, PARTS, S), BF16)
    rest, _ = arena.at(o_p + 4 * PARTS * S // 2, (2, S))
    nmax, o = arena.at(o, (2, 16), BF16)
    cxT, _ = arena.at(o_p, (2, KC, P))
    assert o <= WORDS
    w13_sb, o = arena.at(base, (EXPERTS, KC, 2 * HID))
    w2_sb, o = arena.at(o, (EXPERTS, KC, D))
    b13_sb, o = arena.at(o, (EXPERTS, 2 * HID))
    b2_sb, o = arena.at(o, (EXPERTS, D))
    sw12_sb, o = arena.at(o, (KC, 2 * INNER))
    sw3_sb, o = arena.at(o, (INNER // P, D))
    h13, o = arena.at(o, (4, 2 * HID))
    x2, o = arena.at(o, (4, D))
    prod, o = arena.at(o, (4, D))
    x_in, o = arena.at(o, (4, D))
    xsT, o = arena.at(o, (2, D))
    scaled, _ = arena.at(base, (2, TILES, D))
    act_h, o = arena.at(o, (2, INNER))
    hT, o = arena.at(o, (2, INNER))
    assert o <= WORDS, o
    gate_sb, o = arena.at(o_w, (KC, EXPERTS))
    lower, o = arena.at(o, (EXPERTS, EXPERTS))
    lg, o = arena.at(o, (TILES, EXPERTS))
    mx, o = arena.at(o, (TILES,))
    sc, o = arena.at(o, (TILES, EXPERTS))
    ssum, o = arena.at(o, (TILES,))
    before, o = arena.at(o, (P,))
    steps, o = arena.at(o, (SLOT_TILES,))
    gt, _ = arena.at(base + EXPERTS * KC * 2 * HID, (TILES, EXPERTS * EXPERTS))
    eq, _ = arena.at(base + EXPERTS * KC * 2 * HID + 1024, (TILES, EXPERTS * EXPERTS))
    rank, o = arena.at(o, (TILES, EXPERTS))
    sel, o = arena.at(o, (TILES, EXPERTS))
    sel_k, o = arena.at(o, (2, TILES, EXPERTS))
    run_a, o = arena.at(o, (TILES, EXPERTS))
    run_b, o = arena.at(o, (TILES, EXPERTS))
    total, o = arena.at(o, (TILES, EXPERTS))
    place, o = arena.at(o, (TILES, EXPERTS))
    over, o = arena.at(o, (EXPERTS, TILES))
    n_tiles, o = arena.at(o, (EXPERTS,))
    first, o = arena.at(o, (EXPERTS,))
    last, o = arena.at(o, (EXPERTS,))
    prior, o = arena.at(o, (EXPERTS, EXPERTS))
    tstarts, o = arena.at(o, (TILES,))
    passed, o = arena.at(o, (SLOT_TILES, EXPERTS))
    expert_f, o = arena.at(o, (SLOT_TILES,))
    expert, o = arena.at(o, (SLOT_TILES,), I32)
    pick, o = arena.at(o, (2, TILES, EXPERTS))
    slot_f, o = arena.at(o, (2, TILES))
    slot, o = arena.at(o, (2, TILES), U32)
    weight, o = arena.at(o, (2, TILES))
    assert o <= base

    PS = nc.alloc_psum_tensor("psum", [P, 8, 512], F32)

    made = {}

    def sem(name):
        if name not in made:
            made[name] = nc.alloc_semaphore(name)
        return made[name]

    def bc(ap, shape):
        return ap.broadcast_to(shape)

    x_tiles = x.rearrange("(t p) d -> p t d", p=P)
    out_tiles = out.rearrange("(t p) d -> p t d", p=P)

    def sp_first_loads(sp):
        sp.dma_start(ident, ident_in).then_inc(sem("ident_in"), 16)
        for q in range(4):
            sp.dma_start(xt[:, 4 * q:4 * q + 4], x_tiles[:, 4 * q:4 * q + 4]).then_inc(sem(f"x_in{q}"), 16)
        sp.dma_start(wqk, w_self[0:3].rearrange("w (c p) n -> p w c n", p=P)).then_inc(sem("w_self_in"), 16)
        sp.dma_start(wo_s, w_self[3].rearrange("(c p) n -> p c n", p=P)).then_inc(sem("w_self_in"), 16)
        sp.dma_start(bqk_sb, bqk.rearrange("p (w c) -> p w c", w=2)).then_inc(sem("w_self_in"), 16)
        sp.dma_start(bv_row[0:1], bv).then_inc(sem("w_self_in"), 16)
        for dst, src in ((bo_bc, bo), (ga_bc, gamma), (be_bc, beta)):
            sp.dma_start(dst, src.broadcast_to((P, D))).then_inc(sem("w_self_in"), 16)
    W_SELF = 7 * 16

    def dve_norm(v, n, src, ready, finish):
        for q in range(5):
            if q < 4:
                for t in range(4 * q, 4 * q + 4):
                    ready(v, t)
                for t in range(4 * q, 4 * q + 4):
                    v.bn_stats(stats[:, t], src[:, t]).then_inc(sem("ln_stats"), 1)
                for t in range(4 * q, 4 * q + 4):
                    v.wait_ge(sem("ln_stats"), TILES * n + t + 1)
                    v.bn_aggr(mv[:, t], stats[:, t]).then_inc(sem("ln_var"), 1)
            if q >= 1:
                a, b = 4 * q - 4, 4 * q
                v.wait_ge(sem("ln_std"), 4 * n + q)
                v.reciprocal(rstd[:, a:b], std[:, a:b]).then_inc(sem("ln_rstd"), 1)
                v.wait_ge(sem("ln_rstd"), 4 * n + q)
                finish(v, range(a, b))

    def into(src, dst):
        def finish(v, tiles):
            for t in tiles:
                v.tensor_scalar(dst[:, t], src[:, t], mv[:, t, 0:1], rstd[:, t:t + 1], ALU.subtract,
                                ALU.mult).then_inc(sem("ln_out"), 1)
        return finish

    def act_std(a, n, q):
        a.wait_ge(sem("ln_var"), TILES * n + 4 * q + 4)
        a.activation(std[:, 4 * q:4 * q + 4], mv[:, 4 * q:4 * q + 4, 1], ACT.Sqrt, bias=eps[:, 0:1]) \
            .then_inc(sem("ln_std"), 1)

    def pe_transpose(pe, turn):
        for i in range(8):
            q, c = i // 2, i % 2
            pe.wait_ge(sem("ln_out"), TILES * turn + 4 * q + 4)
            if i >= 4:
                pe.wait_ge(sem("xT"), 8 * turn + i - 3)
            for k in range(4):
                mm = pe.transpose(PS[:, i % 4, P * k:P * k + P], xn[:, 4 * q + k, P * c:P * c + P], ident)
            mm.then_inc(sem("xT_ps"), 1)

    def act_transpose(a, turn):
        for i in range(8):
            act_turned(a, turn, i)

    def act_turned(a, turn, i):
        q, c = i // 2, i % 2
        a.wait_ge(sem("xT_ps"), 8 * turn + i + 1)
        a.copy(xT[:, c, 512 * q:512 * q + 512], PS[:, i % 4, :]).then_inc(sem("xT"), 1)

    def act_norm(a, n, turn):
        for q in range(5):
            if q < 4:
                act_std(a, n, q)
            if q >= 1:
                act_turned(a, turn, 2 * q - 2)
                act_turned(a, turn, 2 * q - 1)

    def times(eng, its):
        return eng.Fori(0, its) if its > 1 else nullcontext(0)

    LOT = 2 * 16

    def pe_split(pe, base, its, plan, before=None, after=None):
        with times(pe, its) as it:
            jobs = plan(it)
            for j, (w, cols, width, bias, _) in enumerate(jobs):
                if before:
                    before(pe, it, j)
                pe.wait_ge(sem("cut_rest"), it * len(jobs) + base + j + 1)
                for c in range(KC):
                    mm = pe.matmul(PS[:, j % 4, 0:width], w(c), cols(c), start=c == 0, stop=c == KC - 1)
                mm.then_inc(sem("cut_ps"), 1)
                if after:
                    after(pe, it, j)

    def act_split(a, base, its, plan, after=None):
        with times(a, its) as it:
            jobs = plan(it)
            for j, (_, _, width, bias, targets) in enumerate(jobs):
                i = it * len(jobs) + base + j
                a.wait_ge(sem("cut_ps"), i + 1)
                a.wait_ge(sem(f"cut_sent{j % 4}"), it * (len(jobs) // 4 * LOT) + (base // 4 + j // 4 + 1) * LOT)
                a.activation(parts[:, j % 4, 0, 0:width], PS[:, j % 4, 0:width], ACT.Identity,
                             bias=0.0 if bias is None else bias).then_inc(sem("cut_hi"), 1)
                a.wait_ge(sem("cut_rest"), i + 5)
                a.copy(parts[:, j % 4, 1, 0:width], rest[:, j % 2, 0:width]).then_inc(sem("cut_mid"), 1)
                if after:
                    after(a, it, j)

    def dve_split(v, base, its, plan):
        if base == 0:
            v.sem_inc(sem("cut_rest"), 4)
        with times(v, its) as it:
            jobs = plan(it)
            for j, (_, _, width, bias, _) in enumerate(jobs):
                i = it * len(jobs) + base + j
                v.wait_ge(sem("cut_hi"), i + 1)
                v.scalar_tensor_tensor(rest[:, j % 2, 0:width], PS[:, j % 4, 0:width],
                                       0.0 if bias is None else bias, parts[:, j % 4, 0, 0:width], ALU.add,
                                       ALU.subtract).then_inc(sem("cut_rest"), 1)
                v.wait_ge(sem("cut_mid"), i + 1)
                v.tensor_tensor(parts[:, j % 4, 2, 0:width], rest[:, j % 2, 0:width], parts[:, j % 4, 1, 0:width],
                                ALU.subtract).then_inc(sem("cut_lo"), 1)

    def sp_split(sp, base, its, plan):
        if base == 0:
            for k in range(4):
                sp.sem_inc(sem(f"cut_sent{k}"), LOT)
        with times(sp, its) as it:
            jobs = plan(it)
            for j, (_, _, width, _, targets) in enumerate(jobs):
                sp.wait_ge(sem("cut_lo"), it * len(jobs) + base + j + 1)
                for p0, p1, dst in targets:
                    sp.dma_start(dst, parts[p0:p1, j % 4, :, 0:width]).then_inc(sem(f"cut_sent{j % 4}"), 16)

    def wait_sent(sp, jobs):
        for k in range(4):
            sp.wait_ge(sem(f"cut_sent{k}"), (jobs // 4 + 1) * LOT)

    def plan_self(it):
        jobs = []
        for half in range(KC):
            for w in range(2):
                rows = qk_self[ds(it, 1), w, :, half * P:half * P + P, :].rearrange("b s p t -> p (b s) t")
                jobs.append((lambda c, w=w, half=half: wqk[:, w, c, half * P:half * P + P],
                             lambda c: xT[:, c, ds(it * S, S)], S, bqk_sb[:, w, half:half + 1],
                             [(0, 64, rows[0:64]), (64, P, rows[64:P])]))
        return jobs

    def two_groups(dst, it, half, lo, width):
        return [(64 * g, 64 * g + 64,
                 dst[ds(it * 4 + 2 * half + g, 1), :, :, lo:lo + width].rearrange("b s p t -> p (b s) t"))
                for g in range(2)]

    def plan_q(it):
        jobs = []
        for b in range(2):
            for half in range(KC):
                jobs.append((lambda c, half=half: wx[:, 0, c, half * P:half * P + P],
                             lambda c, b=b: xT[:, c, ds(it * (2 * S) + b * S, S)], S, None,
                             two_groups(q_cross, it * 2 + b, half, 0, S)))
        return jobs

    def plan_k(it):
        jobs = []
        for b in range(2):
            for half in range(KC):
                for k0 in range(0, SK, KB):
                    n = min(KB, SK - k0)
                    jobs.append((lambda c, half=half: wx[:, 1, c, half * P:half * P + P],
                                 lambda c, b=b, k0=k0, n=n: ctx_sb[:, b, c, k0:k0 + n], n, None,
                                 two_groups(k_cross, it * 2 + b, half, k0, n)))
        return jobs

    J_SELF, J_K, J_Q = 4 * B, 8 * B, 2 * B

    def pe_vself(pe):
        for t in range(TILES):
            bank, off = (t // 2) % 8, (t % 2) * D
            if t == 0:
                pe.wait_ge(sem("constants"), 1)
                pe.wait_ge(sem("cut_rest"), 4 + J_SELF)
            for c in range(KC):
                pe.matmul(PS[:, bank, off:off + D], xT[:, c, P * t:P * t + P], wqk[:, 2, c, :], start=c == 0,
                          stop=False)
            mm = pe.matmul(PS[:, bank, off:off + D], ones[0:1, :], bv_row[0:1, :], start=False, stop=True)
            if t % 8 == 7:
                mm.then_inc(sem("vself_ps"), 1)

    def move_vself(e, copy, done, mine):
        for half in range(2):
            e.wait_ge(sem("vself_ps"), half + 1)
            for gh in (2 * mine, 2 * mine + 1):
                for g in range(4):
                    src = PS[32 * gh:32 * gh + 32, 4 * half:4 * half + 4, :].rearrange(
                        "p k (t j g d) -> p (k t) j g d", t=2, j=ST, g=4)[:, :, :, g]
                    dst = vself[32 * g:32 * g + 32, 8 * half:8 * half + 8, gh]
                    copy(dst, src).then_inc(done, 1)

    class Attention:
        def __init__(self, n, kind, shifted):
            self.n, self.kind, self.rows, self.shifted = n, kind, ROWS + shifted, shifted
            self.selfa = kind == "self"
            self.tiles = ST if self.selfa else XT
            self.its = 2 if self.selfa else 8
            self.per = GROUPS // self.its
            self.block = 4 if self.selfa else 1
            self.halves = 2 * self.per * self.tiles
            self.steps = 4 if self.selfa else 6
            self.dmas = (6 if self.selfa else 12) + shifted

        def s(self, name):
            return sem(f"{self.n}_{name}")

        def keys(self, j):
            return P if self.selfa or j < XT - 1 else XLAST

        def k_tile(self, gl, gh, j):
            if self.selfa:
                return kx_s[0:self.rows, gl // 4, 4 * (gl % 4) + gh, P * j:P * j + P]
            return kx_c[0:self.rows, gl % 2, gh, P * j:P * j + self.keys(j)]

        def queries(self, gl, gh):
            if self.selfa:
                t0 = P * (gl % 4) + 32 * gh
                return qx_s[0:self.rows, gl // 4, :, t0:t0 + 32]
            return qx_c[0:self.rows, gl % 2, gh, :]

        def loads(self, sp, it, k, rows_free):
            blocks = self.per // self.block
            blk = it * blocks + k
            sp.wait_ge(rows_free, blk + 1)
            if self.shifted:
                src = m_self[ds(blk, 1)] if self.selfa else m_cross[ds(blk, 1)]
                dst = (qx_s if self.selfa else qx_c)[ROWS:ROWS + 1, k]
                sp.dma_start(dst, src).then_inc(self.s(f"loaded{k}"), 16)
            for w, of in ((0, Q_PART), (1, K_PART)):
                if w and self.selfa:
                    sp.wait_ge(self.s("ordered"), blk + 1)
                for r in range(6):
                    rows, part = slice(HD * r, HD * r + HD), of[r]
                    if self.selfa:
                        dst = kraw[rows] if w else qx_s[rows, k]
                        src = qk_self[ds(blk, 1), w, part].rearrange("b (c d) t -> (b d) c t", d=HD)
                    elif w == 0:
                        dst = qx_c[rows, k]
                        src = q_cross[ds(blk, 1), part].rearrange("b (g d) t -> (b d) g t", d=HD)
                    else:
                        dst = kx_c[rows, k, :, 0:SK]
                        src = k_cross[ds(blk, 1), part, :, 0:SK].rearrange("b (g d) t -> (b d) g t", d=HD)
                    sp.dma_start(dst, src).then_inc(self.s("kraw") if w and self.selfa else self.s(f"loaded{k}"), 16)

        def order(self, eng, blk, k):
            eng.wait_ge(self.s("kraw"), blk * 96 + 96)
            eng.wait_ge(self.s("rows_free"), blk + 1)
            if eng is nc.gpsimd:
                eng.sem_inc(sem("pool_turn"), 1)
            eng.tensor_copy(kx_s[0:ROWS, k].rearrange("p h (c r) -> p c h r", r=32),
                            kraw[0:ROWS].rearrange("p c (h r) -> p c h r", r=32)).then_inc(self.s("ordered"), 1)

        def sp(self, sp):
            with sp.Fori(0, self.its) as it:
                for k in range(self.per // self.block):
                    self.loads(sp, it, k, self.s("rows_free"))
            if self.selfa:
                sp.wait_ge(self.s("ordered"), B + 1)
                for r in range(6):
                    sp.dma_start(kraw[HD * r:HD * r + HD],
                                 qk_self[B - 1, 1, K_PART[r]].rearrange("(c d) t -> d c t", d=HD)) \
                        .then_inc(self.s("kraw"), 16)

        def pool(self, pool):
            with pool.Fori(0, self.its) as it:
                for gl in range(self.per):
                    pool.wait_ge(self.s("u_free"), it * self.per + gl + 1)
                    if self.selfa:
                        src = vself[:, ds(it * self.per + gl, 1)].rearrange("p a h j d -> p (a h) j d")
                        dst = vg[:, gl % 2, 0:ST, :, 0:HD].rearrange("p j h d -> p h j d")
                    else:
                        src = vcross[:, ds(it * self.per + gl, 1)].rearrange("p a j (h d) -> p (a j) h d", h=4)
                        dst = vg[:, gl % 2, :, :, 0:HD]
                    pool.sem_inc(sem("pool_turn"), 1)
                    if self.selfa:
                        pool.tensor_copy(dst, src).then_inc(self.s("values"), 1)
                    else:
                        pool.tensor_copy(dst[:, 0:XT - 1], src[:, 0:XT - 1]).then_inc(self.s("values"), 1)
                        pool.tensor_copy(dst[0:XLAST, XT - 1], src[0:XLAST, XT - 1]).then_inc(self.s("values"), 1)

        def pe(self, pe):
            pe.sem_inc(self.s("rows_free"), 2)
            pe.sem_inc(self.s("weighed"), 2)
            with pe.Fori(0, self.its) as it:
                units = [(gl, j) for gl in range(self.per) for j in range(self.tiles)]
                first = it * len(units)
                for u, (gl, j) in enumerate(units):
                    self.scores(pe, it, first + u, u, gl, j)
                    if u > 0:
                        self.weigh(pe, it, first + u - 1, u - 1, *units[u - 1])
                self.weigh(pe, it, first + len(units) - 1, len(units) - 1, *units[-1])

        def buffer(self, h):
            return 1 if h == self.halves - 1 else h % 3

        def since(self, h):
            return next(n for n in range(1, 5) if self.buffer((h - n) % self.halves) == self.buffer(h))

        def scores(self, pe, it, u, lu, gl, j):
            if gl % self.block == 0 and j == 0:
                pe.wait_ge(self.s(f"loaded{gl // self.block}"), it * (16 * self.dmas) + 16 * self.dmas)
                if self.selfa:
                    pe.wait_ge(self.s("ordered"), it * 2 + gl // 4 + 2)
            for half in range(2):
                pe.wait_ge(self.s("exp"), u * 2 + half + 5 - self.since(2 * lu + half))
                for gh in (2 * half, 2 * half + 1):
                    m = self.keys(j)
                    mm = pe.matmul(PS[0:m, 2 * self.buffer(2 * lu + half) + gh % 2, :], self.k_tile(gl, gh, j), self.queries(gl, gh), start=True,
                                   stop=True)
                mm.then_inc(self.s("scores"), 1)
            if gl % self.block == self.block - 1 and j == self.tiles - 1:
                pe.wait_ge(self.s("scores"), u * 2 + 2)
                pe.sem_inc(self.s("rows_free"), 1)

        def weigh(self, pe, it, u, lu, gl, j):
            g = it * self.per + gl
            if j == 0:
                copies = 1 if self.selfa else 2
                pe.wait_ge(self.s("values"), g * copies + copies)
                pe.wait_ge(self.s("u_free"), g + 1)
            pe.wait_ge(self.s("exp"), u * 2 + 6)
            m = self.keys(j)
            for gh in range(4):
                mm = pe.matmul(PS[32 * gh:32 * gh + 32, 6 + gl % 2, :], vg[0:m, gl % 2, j, gh, :],
                               probs[0:m, lu % 2, gh, :], start=j == 0, stop=j == self.tiles - 1)
            mm.then_inc(self.s("weighed"), 1)

        def act(self, a):
            a.sem_inc(self.s("exp"), 4)
            with a.Fori(0, self.its) as it:
                units = [(gl, j) for gl in range(self.per) for j in range(self.tiles)]
                for lu, (gl, j) in enumerate(units):
                    u = it * len(units) + lu
                    m = self.keys(j)
                    for half in range(2):
                        if half == 0:
                            a.wait_ge(self.s("weighed"), u + 1)
                        a.wait_ge(self.s("scores"), u * 2 + half + 1)
                        b0 = 2 * self.buffer(2 * lu + half)
                        a.activation(probs[0:m, lu % 2, 2 * half:2 * half + 2], PS[0:m, b0:b0 + 2, :],
                                     ACT.Exp, scale=SCALE).then_inc(self.s("exp"), 1)

        def dve(self, v):
            v.sem_inc(self.s("u_free"), 2)
            n = self.steps
            if self.selfa:
                v.sem_inc(self.s("ordered"), 1)
                self.order(v, 0, 0)
            with v.Fori(0, self.its) as it:
                for gl in range(self.per):
                    g = it * self.per + gl
                    b = gl % 2
                    if self.selfa and gl % 4 == 1:
                        self.order(v, it * 2 + (gl // 4 + 1), (gl // 4 + 1) % 2)
                    v.wait_ge(self.s("weighed"), g * self.tiles + self.tiles + 2)
                    v.transpose(turned[:, b], PS[:, 6 + b, :]).then_inc(self.s("u_free"), 1)
                    v.wait_ge(self.s("u_free"), g + 3)
                    blocks = turned[:, b].rearrange("p (c e) -> p c e", e=32)
                    v.reciprocal(recip[:, b], blocks[:, :, HD]).then_inc(self.s("step"), 1)
                    v.tensor_reduce(low[:, ds(g, 1)], blocks[:, :, HD], AX.X, ALU.min).then_inc(self.s("step"), 1)
                    v.tensor_reduce(high[:, ds(g, 1)], turned[:, b], AX.X, ALU.max,
                                    apply_absolute_value=True).then_inc(self.s("step"), 1)
                    v.wait_ge(self.s("step"), g * n + 3)
                    r = bc(recip[:, b].unsqueeze(2), (P, 16, HD))
                    if self.selfa:
                        dst = ctxn[:, ds(g, 1)].rearrange("p a (c e) -> p (a c) e", e=HD)
                        v.tensor_tensor(dst, blocks[:, :, 0:HD], r, ALU.mult).then_inc(self.s("step"), 1)
                    else:
                        dst = normed[:, b].rearrange("p (c e) -> p c e", e=32)[:, :, 0:HD]
                        v.tensor_tensor(dst, blocks[:, :, 0:HD], r, ALU.mult).then_inc(self.s("step"), 1)
                        v.wait_ge(self.s("step"), g * n + 4)
                        v.transpose(back[:, b], normed[:, b]).then_inc(self.s("step"), 1)
                        v.wait_ge(self.s("step"), g * n + 5)
                        v.tensor_copy(cT[:, ds(g, 1)].rearrange("p a n -> p (a n)"), back[:, b]) \
                            .then_inc(self.s("step"), 1)

        def dve_check(self, v, n):
            v.wait_ge(self.s("step"), self.steps * GROUPS)
            if self.selfa:
                v.wait_ge(self.s("ordered"), B + 2)
            v.tensor_reduce(good[:, 0:1], low, AX.X, ALU.min).then_inc(sem(f"{n}_step"), 1)
            v.tensor_reduce(good[:, 1:2], high, AX.X, ALU.max).then_inc(sem(f"{n}_step"), 1)
            v.wait_ge(sem(f"{n}_step"), 2)
            v.tensor_scalar(good[:, 2:3], good[:, 0:1], DEN_LOW, None, ALU.is_ge).then_inc(sem(f"{n}_step"), 1)
            v.wait_ge(sem(f"{n}_step"), 3)
            v.scalar_tensor_tensor(good[:, 3:4], good[:, 1:2], DEN_HIGH, good[:, 2:3], ALU.is_le,
                                   ALU.mult).then_inc(sem(f"{n}_good"), 1)
            v.wait_ge(sem(f"{n}_count"), 1)
            v.tensor_scalar(flag[0:1, 0:1], PS[0:1, 6, 0:1], P - 0.5, None, ALU.is_le).then_inc(sem(f"{n}_flag"), 1)

        def pe_check(self, pe, n):
            pe.wait_ge(sem(f"{n}_good"), 1)
            pe.matmul(PS[0:1, 6, 0:1], good[:, 3:4], ones[:, 0:1], start=True, stop=True).then_inc(sem(f"{n}_count"), 1)

    class Maxima:

        def __init__(self, n, att):
            self.n, self.a = n, att

        def sp(self, sp):
            a = self.a
            with sp.Fori(0, a.its) as it:
                for k in range(a.per // a.block):
                    a.loads(sp, it, k, a.s("rows_free"))
                    for gl in range(k * a.block, (k + 1) * a.block):
                        g = it * a.per + gl
                        sp.wait_ge(a.s("max_read"), g * 16 + 16 + 2)
                        for gh in range(4):
                            if a.selfa:
                                for q in range(4):
                                    dst = m_self[ds(it * (a.per // 4) + k, 1)].rearrange(
                                        "b (qt q) (t r) -> b q r qt t", q=4, r=32)[:, q, :, :, 4 * (gl % 4) + gh]
                                    sp.dma_start(dst.rearrange("b r qt -> (b r) qt"),
                                                 nmax[32 * q:32 * q + 32, gl % 2, 4 * gh:4 * gh + 4]) \
                                        .then_inc(a.s(f"max_out{gl % 2}"), 16)
                            else:
                                dst = m_cross[ds(g, 1), gh].rearrange("b (qt p) -> (b p) qt", p=P)
                                sp.dma_start(dst, nmax[:, gl % 2, 4 * gh:4 * gh + 4]).then_inc(a.s(f"max_out{gl % 2}"), 16)
            per_group = 16 * (16 if a.selfa else 4)
            for p in range(2):
                sp.wait_ge(a.s(f"max_out{p}"), (GROUPS // 2 + 1) * per_group)

        def pe(self, pe):
            a = self.a
            pe.sem_inc(a.s("rows_free"), 2)
            with pe.Fori(0, a.its) as it:
                for gl in range(a.per):
                    if gl % a.block == 0:
                        pe.wait_ge(a.s(f"loaded{gl // a.block}"), it * (16 * a.dmas) + 16 * a.dmas)
                        if a.selfa:
                            pe.wait_ge(a.s("ordered"), it * 2 + gl // 4 + 2)
                    for gh in range(4):
                        for qt in range(4):
                            i = (it * a.per + gl) * 16 + gh * 4 + qt
                            pe.wait_ge(a.s("max_read"), i + 1)
                            if a.selfa:
                                for q in range(4):
                                    t0 = P * (gl % 4) + 32 * gh
                                    mm = pe.matmul(PS[32 * q:32 * q + 32, 4 * (qt % 2), :],
                                                   qx_s[0:ROWS, gl // 4, 4 * qt + q, t0:t0 + 32],
                                                   kx_s[0:ROWS, gl // 4, 4 * (gl % 4) + gh, :], start=True, stop=True)
                            else:
                                for k in range(4):
                                    mm = pe.matmul(PS[:, 4 * (qt % 2) + k, 0:KB],
                                                   qx_c[0:ROWS, gl % 2, gh, P * qt:P * qt + P],
                                                   kx_c[0:ROWS, gl % 2, gh, KB0[k]:KB0[k] + KB], start=True,
                                                   stop=True)
                            mm.then_inc(a.s("max_ps"), 1)
                    if gl % a.block == a.block - 1:
                        pe.wait_ge(a.s("max_ps"), (it * a.per + gl) * 16 + 16)
                        pe.sem_inc(a.s("rows_free"), 1)

        def dve(self, v):
            a = self.a
            nb, wd = (1, S) if a.selfa else (4, KB)
            v.sem_inc(a.s("max_read"), 2)
            per_group = 16 * (16 if a.selfa else 4)
            for p in range(2):
                v.sem_inc(a.s(f"max_out{p}"), per_group)
            with v.Fori(0, a.its) as it:
                for gl in range(a.per):
                    g = it * a.per + gl
                    v.wait_ge(a.s(f"max_out{gl % 2}"), it * (a.per // 2 * per_group) + (gl // 2 + 1) * per_group)
                    for gh in range(4):
                        for qt in range(4):
                            v.wait_ge(a.s("max_ps"), g * 16 + gh * 4 + qt + 1)
                            b0 = 4 * (qt % 2)
                            v.tensor_reduce(nmax[:, gl % 2, 4 * gh + qt:4 * gh + qt + 1], PS[:, b0:b0 + nb, 0:wd],
                                            AX.XY, ALU.max, negate=True).then_inc(a.s("max_read"), 1)

    A_self, A_cross = Attention("sa", "self", 0), Attention("ca", "cross", 0)
    again = {}
    for kind, n in (("self", "s"), ("cross", "c")):
        again[kind] = (Maxima(f"{n}m", Attention(f"{n}m", kind, 0)), Attention(f"{n}b", kind, 1))

    def redo(eng, name, kind, n):
        mx_, at_ = again[kind]
        eng.wait_ge(sem(f"{n}_flag"), 1)
        bad = eng.value_load(flag[0:1, 0:1], min_val=0, max_val=1)
        with eng.If(bad):
            if name == "sp":
                mx_.sp(eng)
                eng.wait_ge(sem(f"{n}_ones"), 1)
                at_.sp(eng)
            elif name == "pe":
                mx_.pe(eng)
                eng.wait_ge(mx_.a.s("max_read"), GROUPS * 16 + 2)
                at_.pe(eng)
                eng.wait_ge(at_.s("step"), at_.steps * GROUPS)
            elif name == "act":
                at_.act(eng)
            elif name == "dve":
                mx_.dve(eng)
                at_.dve(eng)
                eng.wait_ge(at_.s("step"), at_.steps * GROUPS)
            elif name == "pool":
                if kind == "self":
                    eng.sem_inc(mx_.a.s("ordered"), 1)
                    with eng.Fori(0, 2) as it:
                        for k in range(2):
                            mx_.a.order(eng, it * 2 + k, k)
                eng.wait_ge(mx_.a.s("max_ps"), GROUPS * 16)
                k = kx_s if kind == "self" else kx_c
                eng.memset(k[ROWS:ROWS + 1], 1.0).then_inc(sem(f"{n}_ones"), 1)
                eng.wait_ge(sem(f"{n}_ones"), 1)
                at_.pool(eng)
                eng.wait_ge(at_.s("step"), at_.steps * GROUPS)
                if kind == "self":
                    eng.wait_ge(at_.s("ordered"), B + 2)

    def pe_out_self(pe):
        for t in range(TILES):
            if t >= 2:
                pe.wait_ge(sem("so_cxT"), t - 1)
            for c in range(KC):
                mm = pe.transpose(PS[:, t % 2, P * c:P * c + P], ctxn[:, t, P * c:P * c + P], ident)
            mm.then_inc(sem("so_tr"), 1)
            if t >= 1:
                project_self(pe, t - 1)
        project_self(pe, TILES - 1)

    def project_self(pe, t):
        pe.wait_ge(sem("so_cxT"), t + 1)
        if t >= 2:
            pe.wait_ge(sem("so_y"), t - 1)
        for c in range(KC):
            mm = pe.matmul(PS[:, 2 + t % 2, 0:D], cxT[:, t % 2, c, :], wo_s[:, c, :], start=c == 0, stop=c == KC - 1)
        mm.then_inc(sem("so_ps"), 1)

    def act_out_self(a):
        for t in range(TILES):
            a.wait_ge(sem("so_tr"), t + 1)
            if t >= 2:
                a.wait_ge(sem("so_ps"), t - 1)
            a.copy(cxT[:, t % 2], PS[:, t % 2, 0:D].rearrange("p (c t) -> p c t", c=KC)).then_inc(sem("so_cxT"), 1)
            if t >= 6 and t % 4 == 2:
                act_std(a, 1, (t - 6) // 4)
        act_std(a, 1, 3)

    def dve_out_self(v):
        def ready(v, t):
            v.wait_ge(sem("so_ps"), t + 1)
            if t == 0:
                v.wait_ge(sem("biased"), 2)
            v.tensor_tensor(xn[:, t], xn[:, t], PS[:, 2 + t % 2, 0:D], ALU.add).then_inc(sem("so_y"), 1)
            if t % 4 == 3:
                v.wait_ge(sem("so_y"), t + 1)

        def finish(v, tiles):
            for t in tiles:
                v.scalar_tensor_tensor(xn[:, t], xn[:, t], mv[:, t, 0:1], ga_bc, ALU.subtract, ALU.mult) \
                    .then_inc(sem("so_centred"), 1)
            for t in tiles:
                v.wait_ge(sem("so_centred"), t + 1)
                v.scalar_tensor_tensor(xt[:, t], xn[:, t], rstd[:, t:t + 1], xt[:, t], ALU.mult, ALU.add) \
                    .then_inc(sem("x1"), 1)

        dve_norm(v, 1, xn, ready, finish)

    def pe_values(pe, pair):
        pe.wait_ge(sem("w_cross_in"), 16 * 5)
        for i in range(2 * XT):
            b, jt = i // XT, i % XT
            if jt == 0:
                pe.wait_ge(sem(f"ctx_in{b}"), 16 * pair + 16)
            m = P if jt < XT - 1 else XLAST
            if pair or i >= 4:
                pe.wait_ge(sem("vx_out"), 2 * XT * pair + i - 3)
            for c in range(KC):
                mm = pe.matmul(PS[0:m, 4 + i % 4, 0:D], ctx_sb[:, b, c, P * jt:P * jt + m], wx[:, 2, c, :],
                               start=c == 0, stop=c == KC - 1)
            mm.then_inc(sem("vx_ps"), 1)

    def act_values(a, pair):
        for i in range(2 * XT):
            b, jt = i // XT, i % XT
            m = P if jt < XT - 1 else XLAST
            a.wait_ge(sem("vx_ps"), 2 * XT * pair + i + 1)
            a.copy(vcross[0:m, 8 * pair + 4 * b:8 * pair + 4 * b + 4, jt, :],
                   PS[0:m, 4 + i % 4, 0:D].rearrange("p (h d) -> p h d", h=4)).then_inc(sem("vx_out"), 1)

    def pool_cross_loads(pool):
        pool.dma_start(wx, w_cross.rearrange("w (c p) n -> p w c n", p=P)).then_inc(sem("w_cross_in"), 16)
        pool.memset(wox, 0.0).then_inc(sem("wox_zero"), 1)
        pool.wait_ge(sem("wox_zero"), 1)
        wo_rows = wo_cross.rearrange("(a g d) n -> g d a n", g=4, d=HD)
        for g in range(4):
            pool.dma_start(wox[32 * g:32 * g + HD], wo_rows[g]).then_inc(sem("w_cross_in"), 16)
        for b in range(B):
            if b >= 2:
                pool.wait_ge(sem("vx_ps"), XT * (b - 1))
                pool.wait_ge(sem("cut_ps"), J_SELF + 8 * (b - 1))
            pool.dma_start(ctx_sb[:, b % 2], ctxT[b].rearrange("(c p) k -> p c k", p=P)) \
                .then_inc(sem(f"ctx_in{b % 2}"), 16)

    def pe_out_cross(pe):
        for t in range(TILES):
            b = t // 4
            if t >= 4:
                pe.wait_ge(sem("x2"), t - 3)
            for hg in range(4):
                mm = pe.matmul(PS[:, t % 4, 0:D], cT[:, 4 * b + hg, P * (t % 4):P * (t % 4) + P], wox[:, hg, :],
                               start=hg == 0, stop=hg == 3)
            mm.then_inc(sem("co_ps"), 1)

    def dve_out_cross(v, t):
        v.wait_ge(sem("co_ps"), t + 1)
        v.tensor_tensor(xt[:, t], xt[:, t], PS[:, t % 4, 0:D], ALU.add).then_inc(sem("x2"), 1)
        if t % 4 == 3:
            v.wait_ge(sem("x2"), t + 1)

    def moe_loads(pool):
        pool.wait_ge(sem("co_ps"), TILES)
        pool.dma_start(gate_sb, gate.rearrange("(c p) e -> p c e", p=P)).then_inc(sem("gate_in"), 16)
        pool.dma_start(lower, lower_in.rearrange("(o e) f -> o e f", o=1).broadcast_to((P, EXPERTS, EXPERTS))) \
            .then_inc(sem("gate_in"), 16)
        pool.dma_start(before, before_in).then_inc(sem("gate_in"), 16)
        pool.dma_start(steps, steps_in.broadcast_to((P, SLOT_TILES))).then_inc(sem("gate_in"), 16)
        pool.dma_start(sw12_sb, sw12.rearrange("(c p) n -> p c n", p=P)).then_inc(sem("shared_in"), 16)
        pool.dma_start(sw3_sb, sw3.rearrange("(c p) n -> p c n", p=P)).then_inc(sem("shared_in"), 16)
        pool.dma_start(b13_sb, b13.rearrange("(o e) n -> o e n", o=1).broadcast_to((P, EXPERTS, 2 * HID))) \
            .then_inc(sem("experts_in"), 16)
        pool.dma_start(b2_sb, b2.rearrange("(o e) n -> o e n", o=1).broadcast_to((P, EXPERTS, D))) \
            .then_inc(sem("experts_in"), 16)

    def pool_scatter(pool):
        pool.wait_ge(sem("slots"), 1)
        pool.wait_ge(sem("slots_zero"), 16 * 10)
        for t in range(TILES):
            for k in range(2):
                pool.wait_ge(sem("scaled"), 2 * t + k + 1)
                pool.indirect_dma_start(x_slots, bass.IndirectOffsetOnAxis(ap=slot[:, k, t:t + 1], axis=0),
                                        scaled[:, k, t, :], None, bounds_check=SLOT_TILES * P - 1) \
                    .then_inc(sem("scattered"), 16)
        for e in range(EXPERTS):
            if e == 0:
                pool.wait_ge(sem("scattered"), 16 * 2 * TILES)
            pool.dma_start(w13_sb[:, e], w13[e].rearrange("(c p) n -> p c n", p=P)).then_inc(sem("experts_in"), 16)
            pool.dma_start(w2_sb[:, e], w2[e].rearrange("(c p) n -> p c n", p=P)).then_inc(sem("experts_in"), 16)

    def pool_gather(pool):
        for k in range(U):
            pool.wait_ge(sem(f"y_sent{k}"), 16 * (SLOT_TILES // U) + 16)
        pool.wait_ge(sem("ex_down"), SLOT_TILES + 2)
        for t in range(TILES):
            for k in range(2):
                if t >= 4 and k == 0:
                    pool.wait_ge(sem(f"gathered{t % 4}"), t // 4 * 32)
                pool.indirect_dma_start(scaled[:, k, t, :], None, y_slots,
                                        bass.IndirectOffsetOnAxis(ap=slot[:, k, t:t + 1], axis=0),
                                        bounds_check=SLOT_TILES * P - 1).then_inc(sem(f"gathered{t % 4}"), 16)

    def dve_gathered(v, t):
        v.wait_ge(sem(f"gathered{t % 4}"), 32 * (t // 4) + 32)
        v.tensor_tensor(scaled[:, 0, t], scaled[:, 0, t], scaled[:, 1, t], ALU.add).then_inc(sem("pair"), 1)
        v.wait_ge(sem("pair"), t + 1)
        v.tensor_tensor(xt[:, t], xt[:, t], scaled[:, 0, t], ALU.add).then_inc(sem("final"), 1)

    def pe_route(pe):
        pe.wait_ge(sem("gate_in"), 64)
        pe.wait_ge(sem("xT"), 24)
        for t in range(TILES):
            for c in range(KC):
                mm = pe.matmul(PS[:, 7, 8 * t:8 * t + 8], xT[:, c, P * t:P * t + P], gate_sb[:, c, :], start=c == 0,
                               stop=c == KC - 1)
        mm.then_inc(sem("route_ps"), 1)

    def pe_count(pe):
        pe.wait_ge(sem("route"), 11)
        s_ = sel.rearrange("p t e -> p (t e)")
        pe.matmul(PS[:, 6, 0:P], before, s_, start=True, stop=True)
        pe.matmul(PS[:, 6, P:2 * P], ones, s_, start=True, stop=True).then_inc(sem("route_ps"), 1)

    def dve_route(v):
        E = EXPERTS
        st = [0]
        tile_starts = tstarts

        def done(ins):
            st[0] += 1
            ins.then_inc(sem("route"), 1)
            v.wait_ge(sem("route"), st[0])

        v.wait_ge(sem("gate_in"), 64)
        v.tensor_scalar(tstarts, steps[:, 0:TILES], float(P), None, ALU.mult).then_inc(sem("route_gt"), 1)
        v.wait_ge(sem("route_ps"), 1)
        done(v.tensor_copy(lg, PS[:, 7, 0:E * TILES].rearrange("p (t e) -> p t e", e=E)))
        done(v.tensor_reduce(mx, lg, AX.X, ALU.max))
        done(v.tensor_tensor(lg, lg, bc(mx.unsqueeze(2), (P, TILES, E)), ALU.subtract))
        v.wait_ge(sem("route_exp"), 1)
        done(v.tensor_reduce(ssum, sc, AX.X, ALU.add))
        done(v.reciprocal(ssum, ssum))
        done(v.tensor_tensor(sc, sc, bc(ssum.unsqueeze(2), (P, TILES, E)), ALU.mult))
        gt4 = gt.rearrange("p t (e f) -> p t e f", f=E)
        eq4 = eq.rearrange("p t (e f) -> p t e f", f=E)
        for e in range(E):
            me = bc(sc[:, :, e:e + 1], (P, TILES, E))
            v.tensor_tensor(gt4[:, :, e, :], sc, me, ALU.is_gt).then_inc(sem("route_gt"), 1)
            v.tensor_tensor(eq4[:, :, e, :], sc, me, ALU.is_equal).then_inc(sem("route_gt"), 1)
        v.wait_ge(sem("route_gt"), 2 * E + 1)
        done(v.tensor_tensor(eq, eq, bc(lower.rearrange("p e f -> p (e f)").unsqueeze(1), (P, TILES, E * E)),
                             ALU.mult))
        done(v.tensor_tensor(gt, gt, eq, ALU.add))
        done(v.tensor_reduce(rank, gt4, AX.X, ALU.add))
        done(v.tensor_scalar(sel, rank, 1.5, None, ALU.is_lt))
        for k in range(2):
            done(v.tensor_scalar(sel_k[:, k], rank, float(k), None, ALU.is_equal))
        v.wait_ge(sem("route_ps"), 2)
        done(v.tensor_copy(total, PS[:, 6, P:2 * P].rearrange("p (t e) -> p t e", e=E)))
        src = total
        for step, dst in ((1, run_a), (2, run_b), (4, run_a), (8, run_b)):
            v.tensor_copy(dst[:, 0:step], src[:, 0:step]).then_inc(sem("route"), 1)
            v.tensor_tensor(dst[:, step:], src[:, step:], src[:, 0:TILES - step], ALU.add).then_inc(sem("route"), 1)
            st[0] += 2
            v.wait_ge(sem("route"), st[0])
            src = dst
        full = src[:, TILES - 1, :]
        done(v.tensor_tensor(over, bc(full.unsqueeze(2), (P, E, TILES)), bc(tile_starts.unsqueeze(1), (P, E, TILES)),
                             ALU.is_gt))
        done(v.tensor_reduce(n_tiles, over, AX.X, ALU.add))
        done(v.tensor_tensor(prior, lower, bc(n_tiles.unsqueeze(1), (P, E, E)), ALU.mult))
        done(v.tensor_reduce(first, prior, AX.X, ALU.add))
        done(v.tensor_tensor(last, first, n_tiles, ALU.add))
        done(v.tensor_tensor(place, src, total, ALU.subtract))
        done(v.tensor_tensor(place, place, PS[:, 6, 0:P].rearrange("p (t e) -> p t e", e=E), ALU.add))
        done(v.scalar_tensor_tensor(place, bc(first.unsqueeze(1), (P, TILES, E)), float(P), place, ALU.mult, ALU.add))
        for k in range(2):
            done(v.tensor_tensor(pick[:, k], sel_k[:, k], place, ALU.mult))
        done(v.tensor_reduce(slot_f, pick, AX.X, ALU.add))
        v.tensor_copy(slot, slot_f).then_inc(sem("slots"), 1)
        for k in range(2):
            done(v.tensor_tensor(pick[:, k], sel_k[:, k], sc, ALU.mult))
        done(v.tensor_reduce(weight, pick, AX.X, ALU.add))
        for t in range(TILES):
            for k in range(2):
                v.tensor_scalar(scaled[:, k, t], xn[:, t], weight[:, k, t:t + 1], None, ALU.mult) \
                    .then_inc(sem("scaled"), 1)
        done(v.tensor_tensor(passed, bc(last.unsqueeze(1), (P, SLOT_TILES, E)), bc(steps.unsqueeze(2), (P, SLOT_TILES, E)),
                             ALU.is_le))
        done(v.tensor_reduce(expert_f, passed, AX.X, ALU.add))
        done(v.tensor_scalar(expert_f, expert_f, float(E - 1), None, ALU.min))
        v.tensor_copy(expert, expert_f).then_inc(sem("expert_ids"), 1)

    def act_route(a):
        a.wait_ge(sem("route"), 3)
        a.activation(sc, lg, ACT.Exp).then_inc(sem("route_exp"), 1)

    FIRST, SECOND = range(0, TILES // 2), range(TILES // 2, TILES)

    def pe_shared(pe, part):
        pe.wait_ge(sem("shared_in"), 32)

        def up(t):
            if t >= 2:
                pe.wait_ge(sem("sh_z"), t - 1)
            for h in range(2):
                for c in range(KC):
                    mm = pe.matmul(PS[:, 2 * (t % 2) + h, :], xT[:, c, P * t:P * t + P],
                                   sw12_sb[:, c, 512 * h:512 * h + 512], start=c == 0, stop=c == KC - 1)
            mm.then_inc(sem("sh_up"), 1)

        def turn(t):
            pe.wait_ge(sem("sh_z"), t + 1)
            for k in range(4):
                mm = pe.transpose(PS[:, 4 + t % 2, P * k:P * k + P], act_h[:, t % 2, P * k:P * k + P], ident)
            mm.then_inc(sem("sh_tr"), 1)

        def down(t):
            pe.wait_ge(sem("sh_zT"), t + 1)
            if t >= 2:
                pe.wait_ge(sem("sh_y"), t - 1)
            for k in range(4):
                mm = pe.matmul(PS[:, 6 + t % 2, 0:D], hT[:, t % 2, P * k:P * k + P], sw3_sb[:, k, :], start=k == 0,
                               stop=k == 3)
            mm.then_inc(sem("sh_down"), 1)

        a, b = part[0], part[-1] + 1
        for t in range(a, b + 2):
            if t < b:
                up(t)
            if a + 1 <= t <= b:
                turn(t - 1)
            if t >= a + 2:
                down(t - 2)

    def act_shared(a, part):
        lo, hi = part[0], part[-1] + 1
        for t in range(lo, hi + 1):
            if t < hi:
                a.wait_ge(sem("sh_up"), t + 1)
                if t >= 2:
                    a.wait_ge(sem("sh_tr"), t - 1)
                a.activation(act_h[:, t % 2], PS[:, 2 * (t % 2), :], ACT.Silu).then_inc(sem("sh_silu"), 1)
            if t >= lo + 1:
                k = t - 1
                a.wait_ge(sem("sh_tr"), k + 1)
                if k >= 2:
                    a.wait_ge(sem("sh_down"), k - 1)
                a.copy(hT[:, k % 2, 0:INNER], PS[:, 4 + k % 2, :]).then_inc(sem("sh_zT"), 1)

    def dve_shared(v, part, after=None):
        lo, hi = part[0], part[-1] + 1
        for t in range(lo, hi + 2):
            if t < hi:
                v.wait_ge(sem("sh_silu"), t + 1)
                v.tensor_tensor(act_h[:, t % 2], act_h[:, t % 2], PS[:, 2 * (t % 2) + 1, :], ALU.mult) \
                    .then_inc(sem("sh_z"), 1)
            if t >= lo + 2:
                k = t - 2
                v.wait_ge(sem("sh_down"), k + 1)
                v.tensor_tensor(xt[:, k], xt[:, k], PS[:, 6 + k % 2, 0:D], ALU.add).then_inc(sem("sh_y"), 1)

    U = 4

    def pipeline(eng, lead, step):
        for i in range(lead):
            step(i, i % U)
        n = (SLOT_TILES - lead) // U
        with eng.Fori(0, n) as it:
            for k in range(U):
                step(it * U + (lead + k), (lead + k) % U)
        for i in range(lead + n * U, SLOT_TILES + lead):
            step(i, i % U)

    def stage(i, lag):
        return not isinstance(i, int) or 0 <= i - lag < SLOT_TILES

    def pe_experts(pe):
        pe.wait_ge(sem("experts_in"), 16 * (2 * EXPERTS + 2))
        pe.wait_ge(sem("expert_ids"), 1)
        pe.wait_ge(sem("sh_y"), TILES // 2)
        pe.sem_inc(sem("ex_up"), 2)
        pe.sem_inc(sem("ex_tr"), 2)
        pe.sem_inc(sem("ex_down"), 2)
        pe.sem_inc(sem("ex_xin"), 4)

        def step(i, k):
            if stage(i, 0):
                pe.wait_ge(sem(f"x_loaded{k}"), (i - k) * 4 + 16)
                pe.wait_ge(sem("ex_xsT"), i + 1)
                for c in range(KC):
                    mm = pe.transpose(PS[:, 6 + k % 2, P * c:P * c + P], x_in[:, k, P * c:P * c + P], ident)
                mm.then_inc(sem("ex_xin"), 1)
            if stage(i, 1):
                b = (k - 1) % U
                e = pe.value_load(expert[0:1, ds(i - 1, 1)], min_val=0, max_val=EXPERTS - 1)
                pe.wait_ge(sem("ex_xsT"), i + 2)
                pe.wait_ge(sem("ex_h"), i)
                for c in range(KC):
                    mm = pe.matmul(PS[:, b % 2, :], xsT[:, b % 2, P * c:P * c + P],
                                   w13_sb[:, ds(e, 1), c, :].rearrange("p a n -> p (a n)"), start=c == 0,
                                   stop=c == KC - 1)
                mm.then_inc(sem("ex_up"), 1)
            if stage(i, 2):
                b = (k - 2) % U
                pe.wait_ge(sem("ex_silu"), i - 1)
                pe.wait_ge(sem("ex_hT"), i - 1)
                for c in range(2):
                    mm = pe.transpose(PS[:, 2 + b % 2, P * c:P * c + P], act_h[:, b % 2, P * c:P * c + P], ident)
                mm.then_inc(sem("ex_tr"), 1)
            if stage(i, 3):
                b = (k - 3) % U
                e = pe.value_load(expert[0:1, ds(i - 3, 1)], min_val=0, max_val=EXPERTS - 1)
                pe.wait_ge(sem("ex_hT"), i)
                pe.wait_ge(sem("ex_x2"), i - 2)
                for c in range(2):
                    mm = pe.matmul(PS[:, 4 + b % 2, 0:D], hT[:, b % 2, P * c:P * c + P],
                                   w2_sb[:, ds(e, 1), c, :].rearrange("p a n -> p (a n)"), start=c == 0, stop=c == 1)
                mm.then_inc(sem("ex_down"), 1)

        pipeline(pe, 3, step)

    def act_experts(a):
        a.sem_inc(sem("ex_hT"), 2)
        a.sem_inc(sem("ex_xsT"), 2)

        def step(i, k):
            if stage(i, 0):
                a.wait_ge(sem("ex_xin"), i + 5)
                a.wait_ge(sem("ex_up"), i + 1)
                a.copy(xsT[:, k % 2], PS[:, 6 + k % 2, 0:D]).then_inc(sem("ex_xsT"), 1)
            if stage(i, 1):
                b = (k - 1) % U
                a.wait_ge(sem("ex_h"), i + 2)
                a.wait_ge(sem("ex_tr"), i)
                a.activation(act_h[:, b % 2, 0:HID], h13[:, b, 0:HID], ACT.Silu).then_inc(sem("ex_silu"), 1)
            if stage(i, 2):
                b = (k - 2) % U
                a.wait_ge(sem("ex_tr"), i + 1)
                a.wait_ge(sem("ex_down"), i - 1)
                a.copy(hT[:, b % 2, 0:HID], PS[:, 2 + b % 2, 0:HID]).then_inc(sem("ex_hT"), 1)

        pipeline(a, 2, step)

    def dve_experts(v):
        v.wait_ge(sem("expert_ids"), 1)
        v.wait_ge(sem("experts_in"), 32)
        v.sem_inc(sem("ex_h"), 2)
        v.sem_inc(sem("ex_x2"), 2)

        def step(i, k):
            if stage(i, 1):
                b = (k - 1) % U
                e = v.value_load(expert[0:1, ds(i - 1, 1)], min_val=0, max_val=EXPERTS - 1)
                v.wait_ge(sem("ex_up"), i + 2)
                v.wait_ge(sem("ex_prod"), i)
                v.tensor_tensor(h13[:, b], PS[:, b % 2, :], b13_sb[:, ds(e, 1)].rearrange("p a n -> p (a n)"),
                                ALU.add).then_inc(sem("ex_h"), 1)
            if stage(i, 3):
                b = (k - 3) % U
                e = v.value_load(expert[0:1, ds(i - 3, 1)], min_val=0, max_val=EXPERTS - 1)
                v.wait_ge(sem("ex_down"), i)
                v.tensor_tensor(x2[:, b], PS[:, 4 + b % 2, 0:D], b2_sb[:, ds(e, 1)].rearrange("p a n -> p (a n)"),
                                ALU.add).then_inc(sem("ex_x2"), 1)

        pipeline(v, 3, step)

    def pool_experts(pool):
        pool.sem_inc(sem("ex_prod"), 4)
        with pool.Fori(0, SLOT_TILES // U) as it:
            for k in range(U):
                i = it * U + k
                pool.wait_ge(sem("ex_x2"), i + 3)
                pool.wait_ge(sem(f"y_sent{k}"), it * 16 + 16)
                pool.tensor_tensor(prod[:, k], x2[:, k], h13[:, k, HID:2 * HID], ALU.mult) \
                    .then_inc(sem("ex_prod"), 1)

    def sp_experts(sp):
        for k in range(U):
            sp.sem_inc(sem(f"y_sent{k}"), 16)
        sp.wait_ge(sem("scattered"), 16 * 2 * TILES)

        def load(i, k):
            sp.wait_ge(sem("ex_xin"), i + 1)
            sp.dma_start(x_in[:, k], x_slots[ds(i * P, P)]).then_inc(sem(f"x_loaded{k}"), 16)

        def store(i, k):
            sp.wait_ge(sem("ex_prod"), i + 5)
            sp.dma_start(y_slots[ds(i * P, P)], prod[:, k]).then_inc(sem(f"y_sent{k}"), 16)

        for i in range(2 * U):
            load(i, i % U)
        with sp.Fori(0, SLOT_TILES // U - 2) as it:
            for k in range(U):
                load(it * U + (2 * U + k), k)
                store(it * U + k, k)
        for i in range(SLOT_TILES - 2 * U, SLOT_TILES):
            store(i, i % U)

    with nc.allow_non_contiguous_dma(reason="minus the maxima: single values, on the general path only"), \
            nc.Block() as block:

        @block.sync
        def _(sp):
            sp_first_loads(sp)
            sp_split(sp, 0, B, plan_self)
            wait_sent(sp, J_SELF)
            A_self.sp(sp)
            redo(sp, "sp", "self", "scheck")
            sp_split(sp, J_SELF, 1, plan_k)
            sp_split(sp, J_SELF + J_K // 2, 1, lambda it: plan_k(it + 1))
            sp_split(sp, J_SELF + J_K, 2, plan_q)
            wait_sent(sp, J_SELF + J_K + J_Q)
            sp.wait_ge(sem("vx_ps"), B * XT)
            A_cross.sp(sp)
            redo(sp, "sp", "cross", "ccheck")
            sp_experts(sp)
            for t in range(TILES):
                sp.wait_ge(sem("final"), t + 1)
                sp.dma_start(out_tiles[:, t], xt[:, t]).then_inc(sem("out_sent"), 16)
            sp.wait_ge(sem("out_sent"), 16 * TILES)

        @block.gpsimd
        def _(pool):
            pool.memset(ones, 1.0).then_inc(sem("constants"), 1)
            pool.memset(eps, LN_EPS).then_inc(sem("constants"), 1)
            pool.memset(vg, 1.0).then_inc(sem("constants"), 1)
            pool.memset(normed, 0.0).then_inc(sem("constants"), 1)
            pool.wait_ge(sem("constants"), 4)
            for k in range(10):
                pool.dma_start(x_slots.rearrange("(k p r) d -> k p (r d)", k=10, p=P)[k],
                               normed.rearrange("p a n -> p (a n)")).then_inc(sem("slots_zero"), 16)
            pool.wait_ge(sem("w_self_in"), W_SELF)
            pool.wait_ge(sem("xT"), 8)
            pool.wait_ge(sem("ln_out"), TILES)
            pool.tensor_tensor(xn, xn, bc(bo_bc.unsqueeze(1), (P, TILES, D)), ALU.add).then_inc(sem("biased"), 1)
            pool.tensor_tensor(xt, xt, bc(be_bc.unsqueeze(1), (P, TILES, D)), ALU.add).then_inc(sem("biased"), 1)
            pool.wait_ge(sem("vself_a"), 16)
            pool.wait_ge(sem("vself_b"), 16)
            A_self.pool(pool)
            redo(pool, "pool", "self", "scheck")
            pool_cross_loads(pool)
            pool.wait_ge(sem("vx_out"), B * XT)
            A_cross.pool(pool)
            redo(pool, "pool", "cross", "ccheck")
            moe_loads(pool)
            pool_scatter(pool)
            pool_experts(pool)
            pool_gather(pool)

        @block.vector
        def _(v):
            dve_norm(v, 0, xt, lambda v, t: v.wait_ge(sem(f"x_in{t // 4}"), 16), into(xt, xn))
            dve_split(v, 0, B, plan_self)
            move_vself(v, lambda d, a: v.tensor_copy(d, a), sem("vself_a"), 0)
            A_self.dve(v)
            A_self.dve_check(v, "scheck")
            redo(v, "dve", "self", "scheck")
            dve_out_self(v)
            dve_norm(v, 2, xt, lambda v, t: v.wait_ge(sem("x1"), t + 1), into(xt, xn))
            dve_split(v, J_SELF, 1, plan_k)
            dve_split(v, J_SELF + J_K // 2, 1, lambda it: plan_k(it + 1))
            dve_split(v, J_SELF + J_K, 2, plan_q)
            v.wait_ge(sem("slots_zero"), 16 * 10)
            A_cross.dve(v)
            A_cross.dve_check(v, "ccheck")
            redo(v, "dve", "cross", "ccheck")
            dve_norm(v, 3, xt, dve_out_cross, into(xt, xn))
            dve_route(v)
            dve_shared(v, FIRST)
            dve_experts(v)
            dve_shared(v, SECOND)
            for t in range(TILES):
                dve_gathered(v, t)

        @block.scalar
        def _(a):
            a.wait_ge(sem("constants"), 2)
            act_norm(a, 0, 0)
            a.wait_ge(sem("w_self_in"), W_SELF)
            act_split(a, 0, B, plan_self)
            move_vself(a, lambda d, s_: a.copy(d, s_), sem("vself_b"), 1)
            A_self.act(a)
            redo(a, "act", "self", "scheck")
            act_out_self(a)
            act_values(a, 0)
            for q in range(4):
                act_std(a, 2, q)
            act_split(a, J_SELF, 1, plan_k)
            act_values(a, 1)
            act_split(a, J_SELF + J_K // 2, 1, lambda it: plan_k(it + 1))
            act_transpose(a, 1)
            act_split(a, J_SELF + J_K, 2, plan_q)
            A_cross.act(a)
            redo(a, "act", "cross", "ccheck")
            act_norm(a, 3, 2)
            act_route(a)
            act_shared(a, FIRST)
            act_experts(a)
            act_shared(a, SECOND)

        @block.tensor
        def _(pe):
            pe.wait_ge(sem("ident_in"), 16)
            pe_transpose(pe, 0)
            pe.wait_ge(sem("w_self_in"), W_SELF)
            pe.wait_ge(sem("xT"), 8)
            pe_split(pe, 0, B, plan_self)
            pe_vself(pe)
            pe.wait_ge(sem("vself_a"), 16)
            pe.wait_ge(sem("vself_b"), 16)
            A_self.pe(pe)
            A_self.pe_check(pe, "scheck")
            redo(pe, "pe", "self", "scheck")
            pe.wait_ge(A_self.s("step"), A_self.steps * GROUPS)
            pe_out_self(pe)
            pe.wait_ge(sem("so_y"), TILES)
            pe_values(pe, 0)
            pe_split(pe, J_SELF, 1, plan_k)
            pe_values(pe, 1)
            pe_split(pe, J_SELF + J_K // 2, 1, lambda it: plan_k(it + 1))
            pe.wait_ge(sem("cut_rest"), 4 + J_SELF + J_K)
            pe_transpose(pe, 1)
            pe.wait_ge(sem("xT"), 16)
            pe_split(pe, J_SELF + J_K, 2, plan_q)
            pe.wait_ge(sem("cut_rest"), 4 + J_SELF + J_K + J_Q)
            pe.wait_ge(sem("vx_out"), B * XT)
            A_cross.pe(pe)
            A_cross.pe_check(pe, "ccheck")
            redo(pe, "pe", "cross", "ccheck")
            pe.wait_ge(A_cross.s("step"), A_cross.steps * GROUPS)
            pe_out_cross(pe)
            pe.wait_ge(sem("x2"), TILES)
            pe_transpose(pe, 2)
            pe_route(pe)
            pe_count(pe)
            pe_shared(pe, FIRST)
            pe_experts(pe)
            pe_shared(pe, SECOND)


def kernel(x, ctx_1024, L0_attn_wq, L0_attn_bq, L0_attn_wk, L0_attn_bk, L0_attn_wv, L0_attn_bv, L0_attn_wo,
           L0_attn_bo, L0_attn_gamma, L0_attn_beta, L0_xattn_Wq, L0_xattn_Wk, L0_xattn_Wv, L0_xattn_Wo,
           L0_ffn_gate_w, L0_ffn_w1, L0_ffn_b1, L0_ffn_w2, L0_ffn_b2, L0_ffn_w3, L0_ffn_b3, L0_ffn_sw1,
           L0_ffn_sw2, L0_ffn_sw3):
    import concourse.bacc as bacc
    from concourse.bass_utils import run_bass_kernel_spmd

    def lay(a):
        return np.ascontiguousarray(np.asarray(a))

    a = {k: np.asarray(v) for k, v in locals().items() if k[0] in "xcL"}
    arrays = {
        "x": lay(a["x"].reshape(TOK, D)),
        "ctxT": lay(a["ctx_1024"].transpose(0, 2, 1)),
        "w_self": lay(np.stack([a["L0_attn_wq"], a["L0_attn_wk"], a["L0_attn_wv"], a["L0_attn_wo"]])),
        "bqk": lay(np.stack([a["L0_attn_bq"], a["L0_attn_bk"]]).reshape(4, P).T),
        "bv": lay(a["L0_attn_bv"].reshape(1, D)),
        "bo": lay(a["L0_attn_bo"].reshape(1, D)),
        "gamma": lay(a["L0_attn_gamma"].reshape(1, D)),
        "beta": lay(a["L0_attn_beta"].reshape(1, D)),
        "w_cross": lay(np.stack([a["L0_xattn_Wq"].T, a["L0_xattn_Wk"].T, a["L0_xattn_Wv"].T])),
        "wo_cross": lay(a["L0_xattn_Wo"].T),
        "gate": lay(a["L0_ffn_gate_w"].T),
        "w13": lay(np.concatenate([a["L0_ffn_w1"].transpose(0, 2, 1), a["L0_ffn_w3"].transpose(0, 2, 1)], axis=2)),
        "b13": lay(np.concatenate([a["L0_ffn_b1"], a["L0_ffn_b3"]], axis=1)),
        "w2": lay(a["L0_ffn_w2"].transpose(0, 2, 1)),
        "b2": lay(a["L0_ffn_b2"]),
        "sw12": lay(np.concatenate([a["L0_ffn_sw1"].T, a["L0_ffn_sw2"].T], axis=1)),
        "sw3": lay(a["L0_ffn_sw3"].T),
        "ident_in": np.eye(P, dtype=np.float32),
        "lower_in": np.tril(np.ones((EXPERTS, EXPERTS), np.float32), -1),
        "before_in": np.triu(np.ones((P, P), np.float32), 1),
        "steps_in": np.arange(SLOT_TILES, dtype=np.float32).reshape(1, SLOT_TILES),
    }
    nc = bacc.Bacc("TRN2", target_bir_lowering=False, num_devices=1)
    args = [nc.dram_tensor(n, v.shape, mybir.dt.from_np(v.dtype), kind="ExternalInput").ap()
            for n, v in arrays.items()]
    args.append(nc.dram_tensor("out", (TOK, D), F32, kind="ExternalOutput").ap())
    build(nc, *args)
    r = run_bass_kernel_spmd(nc, [arrays], core_ids=[0])
    return r.results[0]["out"].reshape(B, S, D)
```

```python
from contextlib import nullcontext

import numpy as np
import concourse.bass as bass
from concourse import mybir

F32 = mybir.dt.float32
F32R = mybir.dt.float32r
BF16 = mybir.dt.bfloat16
I32 = mybir.dt.int32
U32 = mybir.dt.uint32
ACT = mybir.ActivationFunctionType
ALU = mybir.AluOpType
AX = mybir.AxisListType
ds = bass.ds

P = 128
B, S, D = 4, 512, 256
SK = 1601
HEADS, HD = 16, 16
TOK = B * S
TILES = TOK // P
KC = D // P
SKP = 1664
XT = (SK + P - 1) // P
XLAST = SK - (XT - 1) * P
KB = 401
KB0 = [0, KB, 2 * KB, SK - KB]
ST = S // P
GROUPS = 16
PARTS = 3
ROWS = 6 * HD
Q_PART = [0, 1, 2, 0, 1, 0]
K_PART = [0, 0, 0, 1, 1, 2]
EXPERTS, HID, INNER = 8, 256, 512
SLOT_TILES = 40
LN_EPS = 1e-5
SCALE = HD ** -0.5
DEN_LOW, DEN_HIGH = 1e-25, 1e34


class Arena:

    def __init__(self, nc, words):
        self.nc, self.words, self.placed = nc, words, 0
        self.start = -(-nc.sbuf_base // 32) * 32
        nc.alloc_sbuf_tensor("arena", [P, words], F32)

    def at(self, off, shape, dt=F32):
        off = -(-off // 8) * 8
        n = int(np.prod(shape))
        w = n if dt != BF16 else (n + 1) // 2
        assert off + w <= self.words, (off, w, self.words)
        self.placed += 1
        t = self.nc.alloc_sbuf_tensor_at(f"sb{self.placed}", [P, n], dt, offset=self.start + 4 * off)
        names = [f"a{i}" for i in range(len(shape))]
        return t[:, 0:n].rearrange(f"p ({' '.join(names)}) -> p {' '.join(names)}", **dict(zip(names, shape))), off + w


def build(nc, x, ctxT, w_self, bqk, bv, bo, gamma, beta, w_cross, wo_cross, gate, w13, b13, w2, b2, sw12, sw3,
          ident_in, lower_in, before_in, steps_in, out):
    def dram(name, shape, dt):
        return nc.dram_tensor(name, shape, dt, kind="Internal").ap()

    qk_self = dram("qk_self", (B, 2, PARTS, D, S), BF16)
    q_cross = dram("q_cross", (GROUPS, PARTS, 64, S), BF16)
    k_cross = dram("k_cross", (GROUPS, PARTS, 64, SKP), BF16)
    m_self = dram("m_self", (B, HEADS, S), BF16)
    m_cross = dram("m_cross", (GROUPS, 4, S), BF16)

    x_slots = dram("x_slots", (SLOT_TILES * P, D), F32)
    y_slots = dram("y_slots", (SLOT_TILES * P, D), F32)

    WORDS = 53200
    arena = Arena(nc, WORDS)
    xt, o = arena.at(0, (TILES, D))
    o_xn = -(-o // 8) * 8
    xn, o = arena.at(o, (TILES, D))
    xT, o = arena.at(o, (KC, TOK))
    ctxn = xT.rearrange("p c t -> p (c t)").rearrange("p (t d) -> p t d", d=D)
    cT, _ = arena.at(o_xn, (GROUPS, S))
    ident, o = arena.at(o, (P,))
    ones, o = arena.at(o, (P,))
    eps, o = arena.at(o, (1,))
    stats, o = arena.at(o, (TILES, 6))
    mv, o = arena.at(o, (TILES, 2))
    std, o = arena.at(o, (TILES,))
    rstd, o = arena.at(o, (TILES,))
    low, o = arena.at(o, (GROUPS,))
    high, o = arena.at(o, (GROUPS,))
    good, o = arena.at(o, (4,))
    flag, o = arena.at(o, (2,), I32)
    o_turned = o
    turned, o = arena.at(o, (2, S))
    recip, o = arena.at(o, (2, 16))
    normed, o = arena.at(o, (2, S))
    back, o = arena.at(o, (2, S))
    gate_sb, o = arena.at(o, (KC, 32))
    lower, o = arena.at(o, (EXPERTS, EXPERTS))
    before, o = arena.at(o, (P,))
    steps, o = arena.at(o, (SLOT_TILES,))
    o_w = o
    wqk, o = arena.at(o_w, (3, KC, D))
    wo_s, o = arena.at(o, (KC, D))
    wx, o = arena.at(o, (3, KC, D))
    wox, _ = arena.at(o_w, (4, D))
    bqk_sb, o = arena.at(o, (2, KC))
    bo_bc, o = arena.at(o, (D,))
    ga_bc, o = arena.at(o, (D,))
    be_bc, o = arena.at(o, (D,))
    bv_row, o = arena.at(o, (D,))
    base = -(-o // 8) * 8
    vself, o = arena.at(base, (TILES, 4, ST, HD))
    qx_s, o = arena.at(o, (2, HEADS, S), BF16)
    kx_s, o = arena.at(o, (2, HEADS, S), BF16)
    kraw, o = arena.at(o, (HEADS, S), BF16)
    o_p = max(o, base + GROUPS * XT * 64 + 8448)
    vcross, o = arena.at(base, (GROUPS, XT, 64))
    o_kx = o
    kx_c, o = arena.at(o, (2, 4, SK + 1), BF16)
    qx_c, o = arena.at(o, (2, 4, S), BF16)
    ctx_sb, oc = arena.at(o_kx, (2, KC, SK + 1))
    assert max(o, oc) <= o_p
    probs, o = arena.at(o_p, (2, 4, S))
    rest, _ = arena.at(o_p + 6 * S, (2, S))
    cxT, _ = arena.at(o_p, (2, KC, P))
    vg, o = arena.at(o, (2, XT, 4, 32))
    nmax, o = arena.at(o, (2, 16), BF16)
    assert o <= WORDS
    parts, _ = arena.at(o_p - 2 * PARTS * S, (4, PARTS, S), BF16)
    w13_in, _ = arena.at(base, (EXPERTS, KC, 2 * HID))
    w13_lo, o = arena.at(base, (EXPERTS, KC, 2 * HID), F32R)
    scaled, _ = arena.at(o, (TILES, 2, D))
    w13_hi, o = arena.at(o, (EXPERTS, KC, 2 * HID), F32R)
    w2_in, _ = arena.at(o, (EXPERTS, KC, D))
    w2_lo, o = arena.at(o, (EXPERTS, KC, D), F32R)
    w2_hi, _ = arena.at(o_xn, (EXPERTS, KC, D), F32R)
    b13_sb, o = arena.at(o, (EXPERTS, 2 * HID))
    b2_sb, o = arena.at(o, (EXPERTS, D))
    sw12_sb, o = arena.at(o, (KC, 2 * INNER))
    sw3_sb, o = arena.at(o, (INNER // P, D))
    h13, o = arena.at(o, (4, 2 * HID))
    assert o <= WORDS, o
    x_in, o = arena.at(o_turned, (4, D))
    ahead, _ = arena.at(o, (TILES, EXPERTS, EXPERTS))
    x2, o = arena.at(o, (4, D))
    xsT, o = arena.at(o, (2, 2, D), F32R)
    assert o <= o_w
    lg, o = arena.at(o_w, (TILES, EXPERTS))
    mx, o = arena.at(o, (TILES,))
    sc, o = arena.at(o, (TILES, EXPERTS))
    ssum, o = arena.at(o, (TILES,))
    rank, o = arena.at(o, (TILES, EXPERTS))
    sel, o = arena.at(o, (TILES, EXPERTS))
    sel_k, o = arena.at(o, (2, TILES, EXPERTS))
    run_a, o = arena.at(o, (TILES, EXPERTS))
    run_b, o = arena.at(o, (TILES, EXPERTS))
    total, o = arena.at(o, (TILES, EXPERTS))
    place, o = arena.at(o, (TILES, EXPERTS))
    over, o = arena.at(o, (EXPERTS, TILES))
    n_tiles, o = arena.at(o, (EXPERTS,))
    first, o = arena.at(o, (EXPERTS,))
    last, o = arena.at(o, (EXPERTS,))
    prior, o = arena.at(o, (EXPERTS, EXPERTS))
    tstarts, o = arena.at(o, (TILES,))
    passed, o = arena.at(o, (SLOT_TILES, EXPERTS))
    expert_f, o = arena.at(o, (SLOT_TILES,))
    expert, o = arena.at(o, (SLOT_TILES,), I32)
    pick, o = arena.at(o, (2, TILES, EXPERTS))
    slot_f, o = arena.at(o, (2, TILES))
    slot, o = arena.at(o, (2, TILES), U32)
    weight, o = arena.at(o, (2, TILES))
    act_h, o = arena.at(o, (2, INNER))
    hxT, _ = arena.at(o, (2, 2, HID), F32R)
    hT, o = arena.at(o, (2, INNER))
    assert o <= base

    PS = nc.alloc_psum_tensor("psum", [P, 8, 512], F32)

    made = {}

    def sem(name):
        if name not in made:
            made[name] = nc.alloc_semaphore(name)
        return made[name]

    def bc(ap, shape):
        return ap.broadcast_to(shape)

    x_tiles = x.rearrange("(t p) d -> p t d", p=P)
    out_tiles = out.rearrange("(t p) d -> p t d", p=P)

    def sp_first_loads(sp):
        sp.dma_start(ident, ident_in).then_inc(sem("ident_in"), 16)
        for q in range(4):
            sp.dma_start(xt[:, 4 * q:4 * q + 4], x_tiles[:, 4 * q:4 * q + 4]).then_inc(sem(f"x_in{q}"), 16)
        sp.dma_start(wqk, w_self[0:3].rearrange("w (c p) n -> p w c n", p=P)).then_inc(sem("w_self_in"), 16)
        sp.dma_start(wo_s, w_self[3].rearrange("(c p) n -> p c n", p=P)).then_inc(sem("w_self_in"), 16)
        sp.dma_start(bqk_sb, bqk.rearrange("p (w c) -> p w c", w=2)).then_inc(sem("w_self_in"), 16)
        sp.dma_start(bv_row[0:1], bv).then_inc(sem("w_self_in"), 16)
        for dst, src in ((bo_bc, bo), (ga_bc, gamma), (be_bc, beta)):
            sp.dma_start(dst, src.broadcast_to((P, D))).then_inc(sem("w_self_in"), 16)
        sp.wait_ge(sem("constants"), 5)
        sp.dma_start(gate_sb[:, :, 0:EXPERTS], gate.rearrange("(c p) e -> p c e", p=P)).then_inc(sem("gate_in"), 16)
        sp.dma_start(lower, lower_in.rearrange("(o e) f -> o e f", o=1).broadcast_to((P, EXPERTS, EXPERTS))) \
            .then_inc(sem("gate_in"), 16)
        sp.dma_start(before, before_in).then_inc(sem("gate_in"), 16)
        sp.dma_start(steps, steps_in.broadcast_to((P, SLOT_TILES))).then_inc(sem("gate_in"), 16)
    W_SELF = 7 * 16

    def dve_norm(v, n, src, ready, finish):
        for q in range(5):
            if q < 4:
                for t in range(4 * q, 4 * q + 4):
                    ready(v, t)
                for t in range(4 * q, 4 * q + 4):
                    v.bn_stats(stats[:, t], src[:, t]).then_inc(sem("ln_stats"), 1)
                for t in range(4 * q, 4 * q + 4):
                    v.wait_ge(sem("ln_stats"), TILES * n + t + 1)
                    v.bn_aggr(mv[:, t], stats[:, t]).then_inc(sem("ln_var"), 1)
            if q >= 1:
                a, b = 4 * q - 4, 4 * q
                v.wait_ge(sem("ln_std"), 4 * n + q)
                v.reciprocal(rstd[:, a:b], std[:, a:b]).then_inc(sem("ln_rstd"), 1)
                v.wait_ge(sem("ln_rstd"), 4 * n + q)
                finish(v, range(a, b))

    def into(src, dst):
        def finish(v, tiles):
            for t in tiles:
                v.tensor_scalar(dst[:, t], src[:, t], mv[:, t, 0:1], rstd[:, t:t + 1], ALU.subtract,
                                ALU.mult).then_inc(sem("ln_out"), 1)
        return finish

    def act_std(a, n, q):
        a.wait_ge(sem("ln_var"), TILES * n + 4 * q + 4)
        a.activation(std[:, 4 * q:4 * q + 4], mv[:, 4 * q:4 * q + 4, 1], ACT.Sqrt, bias=eps[:, 0:1]) \
            .then_inc(sem("ln_std"), 1)

    def pe_transpose(pe, turn):
        for i in range(8):
            q, c = i // 2, i % 2
            pe.wait_ge(sem("ln_out"), TILES * turn + 4 * q + 4)
            if i >= 4:
                pe.wait_ge(sem("xT"), 8 * turn + i - 3)
            for k in range(4):
                mm = pe.transpose(PS[:, i % 4, P * k:P * k + P], xn[:, 4 * q + k, P * c:P * c + P], ident)
            mm.then_inc(sem("xT_ps"), 1)

    def act_transpose(a, turn):
        for i in range(8):
            act_turned(a, turn, i)

    def act_turned(a, turn, i):
        q, c = i // 2, i % 2
        a.wait_ge(sem("xT_ps"), 8 * turn + i + 1)
        a.copy(xT[:, c, 512 * q:512 * q + 512], PS[:, i % 4, :]).then_inc(sem("xT"), 1)

    def act_norm(a, n, turn):
        for q in range(5):
            if q < 4:
                act_std(a, n, q)
            if q >= 1:
                act_turned(a, turn, 2 * q - 2)
                act_turned(a, turn, 2 * q - 1)

    def times(eng, its):
        return eng.Fori(0, its) if its > 1 else nullcontext(0)

    LOT = 2 * 16

    def pe_split(pe, base, its, plan, before=None):
        with times(pe, its) as it:
            jobs = plan(it)
            for j, (w, cols, width, bias, _) in enumerate(jobs):
                if before:
                    before(pe, it, j)
                pe.wait_ge(sem("cut_rest"), it * len(jobs) + base + j + 1)
                for c in range(KC):
                    mm = pe.matmul(PS[:, j % 4, 0:width], w(c), cols(c), start=c == 0, stop=c == KC - 1)
                mm.then_inc(sem("cut_ps"), 1)

    def act_split(a, base, its, plan):
        with times(a, its) as it:
            jobs = plan(it)
            for j in range(len(jobs) + 1):
                if j < len(jobs):
                    _, _, width, bias, _ = jobs[j]
                    a.wait_ge(sem("cut_ps"), it * len(jobs) + base + j + 1)
                    a.wait_ge(sem(f"cut_sent{j % 4}"),
                              it * (len(jobs) // 4 * LOT) + (base // 4 + j // 4 + 1) * LOT)
                    a.activation(parts[:, j % 4, 0, 0:width], PS[:, j % 4, 0:width], ACT.Identity,
                                 bias=0.0 if bias is None else bias).then_inc(sem("cut_hi"), 1)
                if j > 0:
                    i, width = j - 1, jobs[j - 1][2]
                    a.wait_ge(sem("cut_rest"), it * len(jobs) + base + i + 5)
                    a.copy(parts[:, i % 4, 1, 0:width], rest[:, i % 2, 0:width]).then_inc(sem("cut_mid"), 1)

    def dve_split(v, base, its, plan):
        if base == 0:
            v.sem_inc(sem("cut_rest"), 4)
            v.sem_inc(sem("cut_lo"), 2)
        with times(v, its) as it:
            jobs = plan(it)
            for j in range(len(jobs) + 1):
                if j < len(jobs):
                    _, _, width, bias, _ = jobs[j]
                    v.wait_ge(sem("cut_hi"), it * len(jobs) + base + j + 1)
                    v.wait_ge(sem("cut_lo"), it * len(jobs) + base + j + 1)
                    v.scalar_tensor_tensor(rest[:, j % 2, 0:width], PS[:, j % 4, 0:width],
                                           0.0 if bias is None else bias, parts[:, j % 4, 0, 0:width], ALU.add,
                                           ALU.subtract).then_inc(sem("cut_rest"), 1)
                if j > 0:
                    i, width = j - 1, jobs[j - 1][2]
                    v.wait_ge(sem("cut_mid"), it * len(jobs) + base + i + 1)
                    v.tensor_tensor(parts[:, i % 4, 2, 0:width], rest[:, i % 2, 0:width],
                                    parts[:, i % 4, 1, 0:width], ALU.subtract).then_inc(sem("cut_lo"), 1)

    def sp_split(sp, base, its, plan):
        if base == 0:
            for k in range(4):
                sp.sem_inc(sem(f"cut_sent{k}"), LOT)
        with times(sp, its) as it:
            jobs = plan(it)
            for j, (_, _, width, _, targets) in enumerate(jobs):
                sp.wait_ge(sem("cut_lo"), it * len(jobs) + base + j + 3)
                for p0, p1, dst in targets:
                    sp.dma_start(dst, parts[p0:p1, j % 4, :, 0:width]).then_inc(sem(f"cut_sent{j % 4}"), 16)

    def wait_sent(eng, jobs):
        for k in range(4):
            eng.wait_ge(sem(f"cut_sent{k}"), (jobs // 4 + 1) * LOT)

    def plan_self(it):
        jobs = []
        for half in range(KC):
            for w in range(2):
                rows = qk_self[ds(it, 1), w, :, half * P:half * P + P, :].rearrange("b s p t -> p (b s) t")
                jobs.append((lambda c, w=w, half=half: wqk[:, w, c, half * P:half * P + P],
                             lambda c: xT[:, c, ds(it * S, S)], S, bqk_sb[:, w, half:half + 1],
                             [(0, 64, rows[0:64]), (64, P, rows[64:P])]))
        return jobs

    def two_groups(dst, it, half, lo, width):
        return [(64 * g, 64 * g + 64,
                 dst[ds(it * 4 + 2 * half + g, 1), :, :, lo:lo + width].rearrange("b s p t -> p (b s) t"))
                for g in range(2)]

    def plan_q(it):
        jobs = []
        for b in range(2):
            for half in range(KC):
                jobs.append((lambda c, half=half: wx[:, 0, c, half * P:half * P + P],
                             lambda c, b=b: xT[:, c, ds(it * (2 * S) + b * S, S)], S, None,
                             two_groups(q_cross, it * 2 + b, half, 0, S)))
        return jobs

    def plan_k(it):
        jobs = []
        for b in range(2):
            for half in range(KC):
                for k0 in range(0, SK, KB):
                    n = min(KB, SK - k0)
                    jobs.append((lambda c, half=half: wx[:, 1, c, half * P:half * P + P],
                                 lambda c, b=b, k0=k0, n=n: ctx_sb[:, b, c, k0:k0 + n], n, None,
                                 two_groups(k_cross, it * 2 + b, half, k0, n)))
        return jobs

    J_SELF, J_K, J_Q = 4 * B, 8 * B, 2 * B

    def pe_vself(pe):
        pe.wait_ge(sem("constants"), 1)
        for t in (*range(8, TILES), *range(8)):
            bank, off = t // 2, (t % 2) * D
            if t == 0:
                pe.wait_ge(sem("cut_rest"), 4 + J_SELF)
            for c in range(KC):
                pe.matmul(PS[:, bank, off:off + D], xT[:, c, P * t:P * t + P], wqk[:, 2, c, :], start=c == 0,
                          stop=False)
            mm = pe.matmul(PS[:, bank, off:off + D], ones[0:1, :], bv_row[0:1, :], start=False, stop=True)
            if t % 8 == 7:
                mm.then_inc(sem("vself_ps"), 1)

    def move_vself(e, copy, done, mine, turns=(0, 1)):
        for n in turns:
            half = 1 - n
            e.wait_ge(sem("vself_ps"), n + 1)
            for gh in (2 * mine, 2 * mine + 1):
                for g in range(4):
                    src = PS[32 * gh:32 * gh + 32, 4 * half:4 * half + 4, :].rearrange(
                        "p k (t j g d) -> p (k t) j g d", t=2, j=ST, g=4)[:, :, :, g]
                    dst = vself[32 * g:32 * g + 32, 8 * half:8 * half + 8, gh]
                    copy(dst, src).then_inc(done, 1)

    class Attention:
        def __init__(self, n, kind, shifted):
            self.n, self.kind, self.rows, self.shifted = n, kind, ROWS + shifted, shifted
            self.selfa = kind == "self"
            self.tiles = ST if self.selfa else XT
            self.its = 2 if self.selfa else 8
            self.per = GROUPS // self.its
            self.block = 4 if self.selfa else 1
            self.halves = 2 * self.per * self.tiles
            self.steps = 4 if self.selfa else 6
            self.dmas = (6 if self.selfa else 12) + shifted

        def s(self, name):
            return sem(f"{self.n}_{name}")

        def keys(self, j):
            return P if self.selfa or j < XT - 1 else XLAST

        def k_tile(self, gl, gh, j):
            if self.selfa:
                return kx_s[0:self.rows, gl // 4, 4 * (gl % 4) + gh, P * j:P * j + P]
            return kx_c[0:self.rows, gl % 2, gh, P * j:P * j + self.keys(j)]

        def queries(self, gl, gh):
            if self.selfa:
                t0 = P * (gl % 4) + 32 * gh
                return qx_s[0:self.rows, gl // 4, :, t0:t0 + 32]
            return qx_c[0:self.rows, gl % 2, gh, :]

        def loads(self, sp, it, k, rows_free, loaded=None, before_k=None):
            loaded = loaded or self.s(f"loaded{k}")
            blocks = self.per // self.block
            blk = it * blocks + k
            sp.wait_ge(rows_free, blk + 1)
            if self.shifted:
                src = m_self[ds(blk, 1)] if self.selfa else m_cross[ds(blk, 1)]
                dst = (qx_s if self.selfa else qx_c)[ROWS:ROWS + 1, k]
                sp.dma_start(dst, src).then_inc(loaded, 16)
            for w, of in ((0, Q_PART), (1, K_PART)):
                if w and before_k:
                    before_k()
                if w and self.selfa:
                    sp.wait_ge(self.s("ordered"), blk + 1)
                for r in range(6):
                    rows, part = slice(HD * r, HD * r + HD), of[r]
                    if self.selfa:
                        dst = kraw[rows] if w else qx_s[rows, k]
                        src = qk_self[ds(blk, 1), w, part].rearrange("b (c d) t -> (b d) c t", d=HD)
                    elif w == 0:
                        dst = qx_c[rows, k]
                        src = q_cross[ds(blk, 1), part].rearrange("b (g d) t -> (b d) g t", d=HD)
                    else:
                        dst = kx_c[rows, k, :, 0:SK]
                        src = k_cross[ds(blk, 1), part, :, 0:SK].rearrange("b (g d) t -> (b d) g t", d=HD)
                    sp.dma_start(dst, src).then_inc(self.s("kraw") if w and self.selfa else loaded, 16)

        def order(self, eng, blk, k):
            eng.wait_ge(self.s("kraw"), blk * 96 + 96)
            eng.wait_ge(self.s("rows_free"), blk + 1)
            if eng is nc.gpsimd:
                eng.sem_inc(sem("pool_turn"), 1)
            eng.tensor_copy(kx_s[0:ROWS, k].rearrange("p h (c r) -> p c h r", r=32),
                            kraw[0:ROWS].rearrange("p c (h r) -> p c h r", r=32)).then_inc(self.s("ordered"), 1)

        def sp(self, sp, first=True):
            blocks = self.per // self.block
            if not first:
                for k in range(1, blocks):
                    self.loads(sp, 0, k, self.s("rows_free"))
            with sp.Fori(0 if first else 1, self.its) as it:
                for k in range(blocks):
                    self.loads(sp, it, k, self.s("rows_free"))
            if self.selfa:
                sp.wait_ge(self.s("ordered"), B + 1)
                for r in range(6):
                    sp.dma_start(kraw[HD * r:HD * r + HD],
                                 qk_self[B - 1, 1, K_PART[r]].rearrange("(c d) t -> d c t", d=HD)) \
                        .then_inc(self.s("kraw"), 16)

        def pool(self, pool):
            with pool.Fori(0, self.its) as it:
                for gl in range(self.per):
                    pool.wait_ge(self.s("u_free"), it * self.per + gl + 1)
                    if self.selfa:
                        src = vself[:, ds(it * self.per + gl, 1)].rearrange("p a h j d -> p (a h) j d")
                        dst = vg[:, gl % 2, 0:ST, :, 0:HD].rearrange("p j h d -> p h j d")
                    else:
                        src = vcross[:, ds(it * self.per + gl, 1)].rearrange("p a j (h d) -> p (a j) h d", h=4)
                        dst = vg[:, gl % 2, :, :, 0:HD]
                    pool.sem_inc(sem("pool_turn"), 1)
                    if self.selfa:
                        pool.tensor_copy(dst, src).then_inc(self.s("values"), 1)
                    else:
                        pool.tensor_copy(dst[:, 0:XT - 1], src[:, 0:XT - 1]).then_inc(self.s("values"), 1)
                        pool.tensor_copy(dst[0:XLAST, XT - 1], src[0:XLAST, XT - 1]).then_inc(self.s("values"), 1)

        def pe(self, pe):
            if self.shifted:
                pe.sem_inc(self.s("rows_free"), 2)
            pe.sem_inc(self.s("weighed"), 2)
            with pe.Fori(0, self.its) as it:
                units = [(gl, j) for gl in range(self.per) for j in range(self.tiles)]
                first = it * len(units)
                for u, (gl, j) in enumerate(units):
                    self.scores(pe, it, first + u, u, gl, j)
                    if u > 0:
                        self.weigh(pe, it, first + u - 1, u - 1, *units[u - 1])
                self.weigh(pe, it, first + len(units) - 1, len(units) - 1, *units[-1])

        def buffer(self, h):
            return 1 if h == self.halves - 1 else h % 3

        def since(self, h):
            return next(n for n in range(1, 5) if self.buffer((h - n) % self.halves) == self.buffer(h))

        def scores(self, pe, it, u, lu, gl, j):
            if gl % self.block == 0 and j == 0:
                pe.wait_ge(self.s(f"loaded{gl // self.block}"), it * (16 * self.dmas) + 16 * self.dmas)
                if self.selfa:
                    pe.wait_ge(self.s("ordered"), it * 2 + gl // 4 + 2)
            for half in range(2):
                pe.wait_ge(self.s("exp"), u * 2 + half + 5 - self.since(2 * lu + half))
                for gh in (2 * half, 2 * half + 1):
                    m = self.keys(j)
                    mm = pe.matmul(PS[0:m, 2 * self.buffer(2 * lu + half) + gh % 2, :], self.k_tile(gl, gh, j),
                                   self.queries(gl, gh), start=True, stop=True)
                mm.then_inc(self.s("scores"), 1)
            if gl % self.block == self.block - 1 and j == self.tiles - 1:
                pe.wait_ge(self.s("scores"), u * 2 + 2)
                pe.sem_inc(self.s("rows_free"), 1)

        def weigh(self, pe, it, u, lu, gl, j):
            g = it * self.per + gl
            if j == 0:
                copies = 1 if self.selfa else 2
                pe.wait_ge(self.s("values"), g * copies + copies)
                pe.wait_ge(self.s("u_free"), g + 1)
            pe.wait_ge(self.s("exp"), u * 2 + 6)
            m = self.keys(j)
            for gh in range(4):
                mm = pe.matmul(PS[32 * gh:32 * gh + 32, 6 + gl % 2, :], vg[0:m, gl % 2, j, gh, :],
                               probs[0:m, lu % 2, gh, :], start=j == 0, stop=j == self.tiles - 1)
            mm.then_inc(self.s("weighed"), 1)

        def act(self, a):
            a.sem_inc(self.s("exp"), 4)
            with a.Fori(0, self.its) as it:
                units = [(gl, j) for gl in range(self.per) for j in range(self.tiles)]
                for lu, (gl, j) in enumerate(units):
                    u = it * len(units) + lu
                    m = self.keys(j)
                    for half in range(2):
                        if half == 0:
                            a.wait_ge(self.s("weighed"), u + 1)
                        a.wait_ge(self.s("scores"), u * 2 + half + 1)
                        b0 = 2 * self.buffer(2 * lu + half)
                        a.activation(probs[0:m, lu % 2, 2 * half:2 * half + 2], PS[0:m, b0:b0 + 2, :],
                                     ACT.Exp, scale=SCALE).then_inc(self.s("exp"), 1)

        def dve(self, v):
            if self.shifted:
                v.sem_inc(self.s("u_free"), 2)
            n = self.steps
            if self.selfa and self.shifted:
                v.sem_inc(self.s("ordered"), 1)
                self.order(v, 0, 0)
            with v.Fori(0, self.its) as it:
                for gl in range(self.per):
                    g = it * self.per + gl
                    b = gl % 2
                    if self.selfa and gl % 4 == 1:
                        self.order(v, it * 2 + (gl // 4 + 1), (gl // 4 + 1) % 2)
                    v.wait_ge(self.s("weighed"), g * self.tiles + self.tiles + 2)
                    v.transpose(turned[:, b], PS[:, 6 + b, :]).then_inc(self.s("u_free"), 1)
                    v.wait_ge(self.s("u_free"), g + 3)
                    blocks = turned[:, b].rearrange("p (c e) -> p c e", e=32)
                    v.reciprocal(recip[:, b], blocks[:, :, HD]).then_inc(self.s("step"), 1)
                    v.tensor_reduce(low[:, ds(g, 1)], blocks[:, :, HD], AX.X, ALU.min).then_inc(self.s("step"), 1)
                    v.tensor_reduce(high[:, ds(g, 1)], turned[:, b], AX.X, ALU.max,
                                    apply_absolute_value=True).then_inc(self.s("step"), 1)
                    v.wait_ge(self.s("step"), g * n + 3)
                    r = bc(recip[:, b].unsqueeze(2), (P, 16, HD))
                    if self.selfa:
                        dst = ctxn[:, ds(g, 1)].rearrange("p a (c e) -> p (a c) e", e=HD)
                        v.tensor_tensor(dst, blocks[:, :, 0:HD], r, ALU.mult).then_inc(self.s("step"), 1)
                    else:
                        dst = normed[:, b].rearrange("p (c e) -> p c e", e=32)[:, :, 0:HD]
                        v.tensor_tensor(dst, blocks[:, :, 0:HD], r, ALU.mult).then_inc(self.s("step"), 1)
                        v.wait_ge(self.s("step"), g * n + 4)
                        v.transpose(back[:, b], normed[:, b]).then_inc(self.s("step"), 1)
                        v.wait_ge(self.s("step"), g * n + 5)
                        v.tensor_copy(cT[:, ds(g, 1)].rearrange("p a n -> p (a n)"), back[:, b]) \
                            .then_inc(self.s("step"), 1)

        def dve_check(self, v, n):
            v.wait_ge(self.s("step"), self.steps * GROUPS)
            if self.selfa:
                v.wait_ge(self.s("ordered"), B + 2)
            v.tensor_reduce(good[:, 0:1], low, AX.X, ALU.min).then_inc(sem(f"{n}_step"), 1)
            v.tensor_reduce(good[:, 1:2], high, AX.X, ALU.max).then_inc(sem(f"{n}_step"), 1)
            v.wait_ge(sem(f"{n}_step"), 2)
            v.tensor_scalar(good[:, 2:3], good[:, 0:1], DEN_LOW, None, ALU.is_ge).then_inc(sem(f"{n}_step"), 1)
            v.wait_ge(sem(f"{n}_step"), 3)
            v.scalar_tensor_tensor(good[:, 3:4], good[:, 1:2], DEN_HIGH, good[:, 2:3], ALU.is_le,
                                   ALU.mult).then_inc(sem(f"{n}_good"), 1)
            v.wait_ge(sem(f"{n}_count"), 1)
            v.tensor_scalar(flag[0:1, 0:1], PS[0:1, 6, 0:1], P - 0.5, None, ALU.is_le).then_inc(sem(f"{n}_flag"), 1)

        def pe_check(self, pe, n):
            pe.wait_ge(sem(f"{n}_good"), 1)
            pe.matmul(PS[0:1, 6, 0:1], good[:, 3:4], ones[:, 0:1], start=True, stop=True).then_inc(sem(f"{n}_count"), 1)

    class Maxima:

        def __init__(self, n, att):
            self.n, self.a = n, att

        def sp(self, sp):
            a = self.a
            with sp.Fori(0, a.its) as it:
                for k in range(a.per // a.block):
                    a.loads(sp, it, k, a.s("rows_free"))
                    for gl in range(k * a.block, (k + 1) * a.block):
                        g = it * a.per + gl
                        sp.wait_ge(a.s("max_read"), g * 16 + 16 + 2)
                        for gh in range(4):
                            if a.selfa:
                                for q in range(4):
                                    dst = m_self[ds(it * (a.per // 4) + k, 1)].rearrange(
                                        "b (qt q) (t r) -> b q r qt t", q=4, r=32)[:, q, :, :, 4 * (gl % 4) + gh]
                                    sp.dma_start(dst.rearrange("b r qt -> (b r) qt"),
                                                 nmax[32 * q:32 * q + 32, gl % 2, 4 * gh:4 * gh + 4]) \
                                        .then_inc(a.s(f"max_out{gl % 2}"), 16)
                            else:
                                dst = m_cross[ds(g, 1), gh].rearrange("b (qt p) -> (b p) qt", p=P)
                                sp.dma_start(dst, nmax[:, gl % 2, 4 * gh:4 * gh + 4]) \
                                    .then_inc(a.s(f"max_out{gl % 2}"), 16)
            per_group = 16 * (16 if a.selfa else 4)
            for p in range(2):
                sp.wait_ge(a.s(f"max_out{p}"), (GROUPS // 2 + 1) * per_group)

        def pe(self, pe):
            a = self.a
            pe.sem_inc(a.s("rows_free"), 2)
            with pe.Fori(0, a.its) as it:
                for gl in range(a.per):
                    if gl % a.block == 0:
                        pe.wait_ge(a.s(f"loaded{gl // a.block}"), it * (16 * a.dmas) + 16 * a.dmas)
                        if a.selfa:
                            pe.wait_ge(a.s("ordered"), it * 2 + gl // 4 + 2)
                    for gh in range(4):
                        for qt in range(4):
                            i = (it * a.per + gl) * 16 + gh * 4 + qt
                            pe.wait_ge(a.s("max_read"), i + 1)
                            if a.selfa:
                                for q in range(4):
                                    t0 = P * (gl % 4) + 32 * gh
                                    mm = pe.matmul(PS[32 * q:32 * q + 32, 4 * (qt % 2), :],
                                                   qx_s[0:ROWS, gl // 4, 4 * qt + q, t0:t0 + 32],
                                                   kx_s[0:ROWS, gl // 4, 4 * (gl % 4) + gh, :], start=True, stop=True)
                            else:
                                for k in range(4):
                                    mm = pe.matmul(PS[:, 4 * (qt % 2) + k, 0:KB],
                                                   qx_c[0:ROWS, gl % 2, gh, P * qt:P * qt + P],
                                                   kx_c[0:ROWS, gl % 2, gh, KB0[k]:KB0[k] + KB], start=True,
                                                   stop=True)
                            mm.then_inc(a.s("max_ps"), 1)
                    if gl % a.block == a.block - 1:
                        pe.wait_ge(a.s("max_ps"), (it * a.per + gl) * 16 + 16)
                        pe.sem_inc(a.s("rows_free"), 1)

        def dve(self, v):
            a = self.a
            nb, wd = (1, S) if a.selfa else (4, KB)
            v.sem_inc(a.s("max_read"), 2)
            per_group = 16 * (16 if a.selfa else 4)
            for p in range(2):
                v.sem_inc(a.s(f"max_out{p}"), per_group)
            with v.Fori(0, a.its) as it:
                for gl in range(a.per):
                    g = it * a.per + gl
                    v.wait_ge(a.s(f"max_out{gl % 2}"), it * (a.per // 2 * per_group) + (gl // 2 + 1) * per_group)
                    for gh in range(4):
                        for qt in range(4):
                            v.wait_ge(a.s("max_ps"), g * 16 + gh * 4 + qt + 1)
                            b0 = 4 * (qt % 2)
                            v.tensor_reduce(nmax[:, gl % 2, 4 * gh + qt:4 * gh + qt + 1], PS[:, b0:b0 + nb, 0:wd],
                                            AX.XY, ALU.max, negate=True).then_inc(a.s("max_read"), 1)

    A_self, A_cross = Attention("sa", "self", 0), Attention("ca", "cross", 0)
    again = {}
    for kind, n in (("self", "s"), ("cross", "c")):
        again[kind] = (Maxima(f"{n}m", Attention(f"{n}m", kind, 0)), Attention(f"{n}b", kind, 1))

    def redo(eng, name, kind, n):
        mx_, at_ = again[kind]
        eng.wait_ge(sem(f"{n}_flag"), 1)
        bad = eng.value_load(flag[0:1, 0:1], min_val=0, max_val=1)
        with eng.If(bad):
            if name == "sp":
                mx_.sp(eng)
                eng.wait_ge(sem(f"{n}_ones"), 1)
                at_.sp(eng)
            elif name == "pe":
                mx_.pe(eng)
                eng.wait_ge(mx_.a.s("max_read"), GROUPS * 16 + 2)
                at_.pe(eng)
                eng.wait_ge(at_.s("step"), at_.steps * GROUPS)
            elif name == "act":
                at_.act(eng)
            elif name == "dve":
                mx_.dve(eng)
                at_.dve(eng)
                eng.wait_ge(at_.s("step"), at_.steps * GROUPS)
            elif name == "pool":
                if kind == "self":
                    eng.sem_inc(mx_.a.s("ordered"), 1)
                    with eng.Fori(0, 2) as it:
                        for k in range(2):
                            mx_.a.order(eng, it * 2 + k, k)
                eng.wait_ge(mx_.a.s("max_ps"), GROUPS * 16)
                k = kx_s if kind == "self" else kx_c
                eng.memset(k[ROWS:ROWS + 1], 1.0).then_inc(sem(f"{n}_ones"), 1)
                eng.wait_ge(sem(f"{n}_ones"), 1)
                at_.pool(eng)
                eng.wait_ge(at_.s("step"), at_.steps * GROUPS)
                if kind == "self":
                    eng.wait_ge(at_.s("ordered"), B + 2)

    def pe_out_self(pe):
        for t in range(TILES):
            if t >= 2:
                pe.wait_ge(sem("so_cxT"), t - 1)
            for c in range(KC):
                mm = pe.transpose(PS[:, t % 2, P * c:P * c + P], ctxn[:, t, P * c:P * c + P], ident)
            mm.then_inc(sem("so_tr"), 1)
            if t >= 1:
                project_self(pe, t - 1)
        project_self(pe, TILES - 1)

    def project_self(pe, t):
        pe.wait_ge(sem("so_cxT"), t + 1)
        if t >= 2:
            pe.wait_ge(sem("so_y"), t - 1)
        for c in range(KC):
            mm = pe.matmul(PS[:, 2 + t % 2, 0:D], cxT[:, t % 2, c, :], wo_s[:, c, :], start=c == 0, stop=c == KC - 1)
        mm.then_inc(sem("so_ps"), 1)

    def act_out_self(a):
        for t in range(TILES):
            a.wait_ge(sem("so_tr"), t + 1)
            if t >= 2:
                a.wait_ge(sem("so_ps"), t - 1)
            a.copy(cxT[:, t % 2], PS[:, t % 2, 0:D].rearrange("p (c t) -> p c t", c=KC)).then_inc(sem("so_cxT"), 1)
            if t >= 6 and t % 4 == 2:
                act_std(a, 1, (t - 6) // 4)
        act_std(a, 1, 3)

    def dve_out_self(v):
        def ready(v, t):
            v.wait_ge(sem("so_ps"), t + 1)
            if t == 0:
                v.wait_ge(sem("constants"), 7)
            v.tensor_tensor(xn[:, t], xn[:, t], PS[:, 2 + t % 2, 0:D], ALU.add).then_inc(sem("so_y"), 1)
            if t % 4 == 3:
                v.wait_ge(sem("so_y"), t + 1)

        def finish(v, tiles):
            for t in tiles:
                v.tensor_scalar(xn[:, t], xn[:, t], mv[:, t, 0:1], rstd[:, t:t + 1], ALU.subtract, ALU.mult) \
                    .then_inc(sem("so_norm"), 1)

        dve_norm(v, 1, xn, ready, finish)

    def pool_out_self(pool):
        for q in range(4):
            pool.wait_ge(sem("so_norm"), 4 * q + 4)
            four = slice(4 * q, 4 * q + 4)
            pool.tensor_tensor(xn[:, four], xn[:, four], bc(ga_bc.unsqueeze(1), (P, 4, D)), ALU.mult) \
                .then_inc(sem("x1"), 1)
            pool.wait_ge(sem("x1"), 2 * q + 1)
            pool.tensor_tensor(xt[:, four], xt[:, four], xn[:, four], ALU.add).then_inc(sem("x1"), 1)

    def pe_values(pe, pair):
        pe.wait_ge(sem("w_cross_in"), 16 * 5)
        for i in range(2 * XT):
            b, jt = i // XT, i % XT
            if jt == 0:
                pe.wait_ge(sem(f"ctx_in{b}"), 16 * pair + 16)
            m = P if jt < XT - 1 else XLAST
            if pair or i >= 4:
                pe.wait_ge(sem("vx_out"), 2 * XT * pair + i - 3)
            for c in range(KC):
                mm = pe.matmul(PS[0:m, 4 + i % 4, 0:D], ctx_sb[:, b, c, P * jt:P * jt + m], wx[:, 2, c, :],
                               start=c == 0, stop=c == KC - 1)
            mm.then_inc(sem("vx_ps"), 1)

    def act_values(a, pair):
        for i in range(2 * XT):
            b, jt = i // XT, i % XT
            m = P if jt < XT - 1 else XLAST
            a.wait_ge(sem("vx_ps"), 2 * XT * pair + i + 1)
            a.copy(vcross[0:m, 8 * pair + 4 * b:8 * pair + 4 * b + 4, jt, :],
                   PS[0:m, 4 + i % 4, 0:D].rearrange("p (h d) -> p h d", h=4)).then_inc(sem("vx_out"), 1)

    def pool_cross_loads(pool):
        pool.dma_start(wx, w_cross.rearrange("w (c p) n -> p w c n", p=P)).then_inc(sem("w_cross_in"), 16)
        pool.memset(wox, 0.0).then_inc(sem("constants"), 1)
        pool.wait_ge(sem("constants"), 8)
        wo_rows = wo_cross.rearrange("(a g d) n -> g d a n", g=4, d=HD)
        for g in range(4):
            pool.dma_start(wox[32 * g:32 * g + HD], wo_rows[g]).then_inc(sem("w_cross_in"), 16)
        for b in range(B):
            if b == 2:
                pool_out_self(pool)
                for q in range(4):
                    pool.wait_ge(sem("ln_rstd"), 4 * 2 + q + 1)
                    into(xt, xn)(pool, range(4 * q, 4 * q + 4))
            if b >= 2:
                pool.wait_ge(sem("vx_ps"), XT * (b - 1))
                pool.wait_ge(sem("cut_ps"), J_SELF + 8 * (b - 1))
            pool.dma_start(ctx_sb[:, b % 2, :, 0:SK], ctxT[b].rearrange("(c p) k -> p c k", p=P)) \
                .then_inc(sem(f"ctx_in{b % 2}"), 16)

    def pe_out_cross(pe):
        for t in range(TILES):
            b = t // 4
            if t >= 4:
                pe.wait_ge(sem("x2"), t - 3)
            for hg in range(4):
                mm = pe.matmul(PS[:, t % 4, 0:D], cT[:, 4 * b + hg, P * (t % 4):P * (t % 4) + P], wox[:, hg, :],
                               start=hg == 0, stop=hg == 3)
            mm.then_inc(sem("co_ps"), 1)

    def dve_out_cross(v, t):
        v.wait_ge(sem("co_ps"), t + 1)
        v.tensor_tensor(xt[:, t], xt[:, t], PS[:, t % 4, 0:D], ALU.add).then_inc(sem("x2"), 1)
        if t % 4 == 3:
            v.wait_ge(sem("x2"), t + 1)

    def moe_loads(sp):
        sp.wait_ge(sem("co_ps"), TILES)
        sp.dma_start(sw12_sb, sw12.rearrange("(c p) n -> p c n", p=P)).then_inc(sem("shared_in"), 16)
        sp.dma_start(sw3_sb, sw3.rearrange("(c p) n -> p c n", p=P)).then_inc(sem("shared_in"), 16)
        for e in range(EXPERTS):
            sp.dma_start(w13_in[:, e], w13[e].rearrange("(c p) n -> p c n", p=P)).then_inc(sem("experts_in"), 16)
            sp.dma_start(w2_in[:, e], w2[e].rearrange("(c p) n -> p c n", p=P)).then_inc(sem("experts_in"), 16)
        sp.dma_start(b13_sb, b13.rearrange("(o e) n -> o e n", o=1).broadcast_to((P, EXPERTS, 2 * HID))) \
            .then_inc(sem("biases_in"), 16)
        sp.dma_start(b2_sb, b2.rearrange("(o e) n -> o e n", o=1).broadcast_to((P, EXPERTS, D))) \
            .then_inc(sem("biases_in"), 16)

    LOTS = 2 * 64

    def pool_scatter(pool):
        pool.wait_ge(sem("slots"), 1)
        pool.wait_ge(sem("slots_zero"), 16 * 10)
        for t in range(TILES):
            lot = t // 2
            if lot >= 4 and t % 2 == 0:
                pool.wait_ge(sem(f"moved{lot % 4}"), 64)
            for k in range(2):
                pool.wait_ge(sem(f"scaled_{k}"), t + 1)
                pool.indirect_dma_start(x_slots, bass.IndirectOffsetOnAxis(ap=slot[:, k, t:t + 1], axis=0),
                                        scaled[:, t, k, :], None, bounds_check=SLOT_TILES * P - 1) \
                    .then_inc(sem(f"moved{lot % 4}"), 16)

    def act_weights(a, e):
        if e == 0:
            a.wait_ge(sem("experts_in"), 16 * 2 * EXPERTS)
            a.wait_ge(sem("scaled_0"), TILES)
            a.wait_ge(sem("scaled_1"), TILES)
        a.wait_ge(sem(f"moved{e % 4}"), 64 * (e // 4) + 64)
        a.copy(w13_hi[:, e], w13_in[:, e]).then_inc(sem("w_hi"), 1)
        a.copy(w2_hi[:, e], w2_in[:, e]).then_inc(sem("w_hi"), 1)

    def dve_weights(v, e):
        v.wait_ge(sem("w_hi"), 2 * e + 2)
        v.tensor_tensor(w13_lo[:, e], w13_in[:, e], w13_hi[:, e].bitcast(F32), ALU.subtract).then_inc(sem("w_lo"), 1)
        v.tensor_tensor(w2_lo[:, e], w2_in[:, e], w2_hi[:, e].bitcast(F32), ALU.subtract).then_inc(sem("w_lo"), 1)

    def pool_gather(pool):
        for k in range(U):
            pool.wait_ge(sem(f"y_sent{k}"), 16 * (SLOT_TILES // U) + 16)
        pool.wait_ge(sem("ex_down"), SLOT_TILES + 2)
        for t in range(TILES):
            for k in range(2):
                if t >= 4 and k == 0:
                    pool.wait_ge(sem(f"moved{t % 4}"), LOTS + t // 4 * 32)
                pool.indirect_dma_start(scaled[:, t, k, :], None, y_slots,
                                        bass.IndirectOffsetOnAxis(ap=slot[:, k, t:t + 1], axis=0),
                                        bounds_check=SLOT_TILES * P - 1).then_inc(sem(f"moved{t % 4}"), 16)

    def dve_gathered(v, t):
        v.wait_ge(sem(f"moved{t % 4}"), LOTS + 32 * (t // 4) + 32)
        v.tensor_tensor(scaled[:, t, 0], scaled[:, t, 0], scaled[:, t, 1], ALU.add).then_inc(sem("pair"), 1)
        v.wait_ge(sem("pair"), t + 1)
        v.tensor_tensor(xt[:, t], xt[:, t], scaled[:, t, 0], ALU.add).then_inc(sem("final"), 1)

    def pe_route(pe):
        pe.wait_ge(sem("gate_in"), 64)
        pe.wait_ge(sem("xT"), 24)
        for c in range(KC):
            for q in range(4):
                mm = pe.matmul(PS[32 * q:32 * q + 32, 7, :], gate_sb[:, c, :],
                               xT[:, c].rearrange("p (t q r) -> p t q r", q=4, r=32)[:, :, q, :], start=c == 0,
                               stop=c == KC - 1)
        mm.then_inc(sem("route_ps"), 1)

    def pe_count(pe):
        pe.wait_ge(sem("route"), 8)
        s_ = sel.rearrange("p t e -> p (t e)")
        pe.matmul(PS[:, 6, 0:P], before, s_, start=True, stop=True)
        pe.matmul(PS[:, 6, P:2 * P], ones, s_, start=True, stop=True).then_inc(sem("route_ps"), 1)

    def dve_route(v):
        E = EXPERTS
        st = [0]

        def done(ins):
            st[0] += 1
            ins.then_inc(sem("route"), 1)
            v.wait_ge(sem("route"), st[0])

        v.wait_ge(sem("gate_in"), 64)
        v.tensor_scalar(tstarts, steps[:, 0:TILES], float(P), None, ALU.mult).then_inc(sem("route_gt"), 1)
        v.memset(ahead, 0.0).then_inc(sem("route_gt"), 1)
        v.wait_ge(sem("route_ps"), 1)
        done(v.transpose(turned[:, 0], PS[:, 7, :]))
        logits = turned[:, 0].rearrange("p (t e) -> p t e", e=32)[:, :, 0:E]
        done(v.tensor_reduce(mx, logits, AX.X, ALU.max))
        done(v.tensor_tensor(lg, logits, bc(mx.unsqueeze(2), (P, TILES, E)), ALU.subtract))
        v.wait_ge(sem("route_exp"), 1)
        done(v.tensor_reduce(ssum, sc, AX.X, ALU.add))
        done(v.reciprocal(ssum, ssum))
        done(v.tensor_tensor(sc, sc, bc(ssum.unsqueeze(2), (P, TILES, E)), ALU.mult))
        v.wait_ge(sem("route_gt"), 2)
        for e in range(E):
            if e > 0:
                v.tensor_tensor(ahead[:, :, e, 0:e], sc[:, :, 0:e], bc(sc[:, :, e:e + 1], (P, TILES, e)), ALU.is_ge) \
                    .then_inc(sem("route_gt"), 1)
            if e < E - 1:
                v.tensor_tensor(ahead[:, :, e, e + 1:], sc[:, :, e + 1:], bc(sc[:, :, e:e + 1], (P, TILES, E - 1 - e)),
                                ALU.is_gt).then_inc(sem("route_gt"), 1)
        dve_up(v, 0)
        v.wait_ge(sem("route_gt"), 2 * E)
        done(v.tensor_reduce(rank, ahead, AX.X, ALU.add))
        done(v.tensor_scalar(sel, rank, 1.5, None, ALU.is_lt))
        dve_up(v, 1)
        for k in range(2):
            done(v.tensor_scalar(sel_k[:, k], rank, float(k), None, ALU.is_equal))
        v.wait_ge(sem("route_ps"), 2)
        done(v.tensor_copy(total, PS[:, 6, P:2 * P].rearrange("p (t e) -> p t e", e=E)))
        done(v.tensor_copy(place, PS[:, 6, 0:P].rearrange("p (t e) -> p t e", e=E)))
        src = total
        for step, dst in ((1, run_a), (2, run_b), (4, run_a), (8, run_b)):
            v.tensor_copy(dst[:, 0:step], src[:, 0:step]).then_inc(sem("route"), 1)
            v.tensor_tensor(dst[:, step:], src[:, step:], src[:, 0:TILES - step], ALU.add).then_inc(sem("route"), 1)
            st[0] += 2
            v.wait_ge(sem("route"), st[0])
            src = dst
        full = src[:, TILES - 1, :]
        done(v.tensor_tensor(over, bc(full.unsqueeze(2), (P, E, TILES)), bc(tstarts.unsqueeze(1), (P, E, TILES)),
                             ALU.is_gt))
        done(v.tensor_reduce(n_tiles, over, AX.X, ALU.add))
        done(v.tensor_tensor(prior, lower, bc(n_tiles.unsqueeze(1), (P, E, E)), ALU.mult))
        done(v.tensor_reduce(first, prior, AX.X, ALU.add))
        done(v.tensor_tensor(last, first, n_tiles, ALU.add))
        done(v.tensor_tensor(place, place, src, ALU.add))
        done(v.tensor_tensor(place, place, total, ALU.subtract))
        done(v.scalar_tensor_tensor(place, bc(first.unsqueeze(1), (P, TILES, E)), float(P), place, ALU.mult, ALU.add))
        for k in range(2):
            done(v.tensor_tensor(pick[:, k], sel_k[:, k], place, ALU.mult))
        done(v.tensor_reduce(slot_f, pick, AX.X, ALU.add))
        v.tensor_copy(slot, slot_f).then_inc(sem("slots"), 1)
        for k in range(2):
            done(v.tensor_tensor(pick[:, k], sel_k[:, k], sc, ALU.mult))
        done(v.tensor_reduce(weight, pick, AX.X, ALU.add))
        v.sem_inc(sem("weights"), 1)
        dve_up(v, 2)
        dve_down(v, 0)
        for t in range(TILES):
            v.tensor_scalar(scaled[:, t, 0], xn[:, t], weight[:, 0, t:t + 1], None, ALU.mult) \
                .then_inc(sem("scaled_0"), 1)
        done(v.tensor_tensor(passed, bc(last.unsqueeze(1), (P, SLOT_TILES, E)),
                             bc(steps.unsqueeze(2), (P, SLOT_TILES, E)), ALU.is_le))
        done(v.tensor_reduce(expert_f, passed, AX.X, ALU.add))
        done(v.tensor_scalar(expert_f, expert_f, float(E - 1), None, ALU.min))
        v.tensor_copy(expert, expert_f).then_inc(sem("expert_ids"), 1)
        dve_up(v, 3)
        dve_down(v, 1)

    def act_route(a):
        a.wait_ge(sem("route"), 3)
        a.activation(sc, lg, ACT.Exp).then_inc(sem("route_exp"), 1)

    def act_scaled(a):
        a.wait_ge(sem("weights"), 1)
        for t in range(TILES):
            a.activation(scaled[:, t, 1], xn[:, t], ACT.Copy, scale=weight[:, 1, t:t + 1]).then_inc(sem("scaled_1"), 1)

    FIRST, SECOND = range(0, 9), range(9, TILES)

    def pe_shared(pe, part, between=None):
        pe.wait_ge(sem("shared_in"), 32)

        def up(t):
            if t >= 2:
                pe.wait_ge(sem("sh_z"), t - 1)
            for h in range(2):
                for c in range(KC):
                    mm = pe.matmul(PS[:, 2 * (t % 2) + h, :], xT[:, c, P * t:P * t + P],
                                   sw12_sb[:, c, 512 * h:512 * h + 512], start=c == 0, stop=c == KC - 1)
            mm.then_inc(sem("sh_up"), 1)

        def turn(t):
            pe.wait_ge(sem("sh_z"), t + 1)
            for k in range(4):
                mm = pe.transpose(PS[:, 4 + t % 2, P * k:P * k + P], act_h[:, t % 2, P * k:P * k + P], ident)
            mm.then_inc(sem("sh_tr"), 1)

        def down(t):
            pe.wait_ge(sem("sh_zT"), t + 1)
            if t == 0:
                pe.wait_ge(sem("route"), 12)
            if t >= 2:
                pe.wait_ge(sem("sh_y"), t - 1)
            for k in range(4):
                mm = pe.matmul(PS[:, 6 + t % 2, 0:D], hT[:, t % 2, P * k:P * k + P], sw3_sb[:, k, :], start=k == 0,
                               stop=k == 3)
            mm.then_inc(sem("sh_down"), 1)

        a, b = part[0], part[-1] + 1
        for t in range(a, b + 2):
            if t < b:
                up(t)
            if between and t == a + 1:
                between(pe)
            if a + 1 <= t <= b:
                turn(t - 1)
            if t >= a + 2:
                down(t - 2)

    def act_gate(a, t):
        a.wait_ge(sem("sh_up"), t + 1)
        if t >= 2:
            a.wait_ge(sem("sh_tr"), t - 1)
        a.activation(act_h[:, t % 2], PS[:, 2 * (t % 2), :], ACT.Silu).then_inc(sem("sh_silu"), 1)

    def act_hidden(a, t):
        a.wait_ge(sem("sh_tr"), t + 1)
        if t >= 2:
            a.wait_ge(sem("sh_down"), t - 1)
        a.copy(hT[:, t % 2, 0:INNER], PS[:, 4 + t % 2, :]).then_inc(sem("sh_zT"), 1)

    def act_shared(a, part):
        lo, hi = part[0], part[-1] + 1
        for t in range(lo, hi + 1):
            if t < hi:
                act_gate(a, t)
            if t > lo:
                act_hidden(a, t - 1)
            if part is FIRST:
                if t == 2:
                    act_scaled(a)
                if t >= 4:
                    act_weights(a, t - 4)
        if part is FIRST:
            for e in range(hi - 3, EXPERTS):
                act_weights(a, e)

    def dve_up(v, t):
        v.wait_ge(sem("sh_silu"), t + 1)
        v.tensor_tensor(act_h[:, t % 2], act_h[:, t % 2], PS[:, 2 * (t % 2) + 1, :], ALU.mult).then_inc(sem("sh_z"), 1)

    def dve_down(v, t):
        v.wait_ge(sem("sh_down"), t + 1)
        v.tensor_tensor(xt[:, t], xt[:, t], PS[:, 6 + t % 2, 0:D], ALU.add).then_inc(sem("sh_y"), 1)

    def dve_shared_first(v):
        n = len(FIRST)
        for t in range(4, n + 2):
            if t < n:
                dve_up(v, t)
            dve_down(v, t - 2)
            dve_weights(v, t - 4)
        for e in range(n - 2, EXPERTS):
            dve_weights(v, e)

    def dve_shared_second(v):
        lo, n, gathered = SECOND[0], len(SECOND), 0
        for i in range(n + 2):
            if i < n:
                dve_up(v, lo + i)
            if i >= 2:
                dve_down(v, lo + i - 2)
            upto = TILES if i == n + 1 else min(TILES * i // n, lo + i - 1)
            for t in range(gathered, upto):
                dve_gathered(v, t)
            gathered = max(gathered, upto)

    U = 4

    def pipeline(eng, lead, step):
        for i in range(lead):
            step(i, i % U)
        n = (SLOT_TILES - lead) // U
        with eng.Fori(0, n) as it:
            for k in range(U):
                step(it * U + (lead + k), (lead + k) % U)
        for i in range(lead + n * U, SLOT_TILES + lead):
            step(i, i % U)

    def stage(i, lag):
        return not isinstance(i, int) or 0 <= i - lag < SLOT_TILES

    def pe_parts(pe, dst, rows, weights, e):
        steps_ = [(c, a, b) for c in range(KC) for a, b in ((0, 0), (1, 0), (0, 1))]
        for n, (c, a, b) in enumerate(steps_):
            mm = pe.matmul(dst, rows[:, a, P * c:P * c + P],
                           weights[b][:, ds(e, 1), c, :].rearrange("p a n -> p (a n)"), start=n == 0,
                           stop=n == len(steps_) - 1)
        return mm

    def load_expert(eng, kept, j, k):
        e = eng.value_load(expert[0:1, ds(j, 1)], min_val=0, max_val=EXPERTS - 1)
        eng.reg_mov(kept[k], e)
        return e

    def kept_expert(eng, kept, k):
        return eng.snap(kept[k], min_val=0, max_val=EXPERTS - 1)

    def pe_experts(pe):
        kept = [pe.alloc_register(f"pe_expert{k}") for k in range(U)]
        pe.wait_ge(sem("w_lo"), 2 * EXPERTS)
        pe.wait_ge(sem("expert_ids"), 1)
        pe.wait_ge(sem("sh_y"), len(FIRST))
        pe.sem_inc(sem("ex_up"), 2)
        pe.sem_inc(sem("ex_tr"), 2)
        pe.sem_inc(sem("ex_down"), 2)
        pe.sem_inc(sem("ex_xin"), 4)

        def step(i, k):
            if stage(i, 0):
                pe.wait_ge(sem(f"x_loaded{k}"), (i - k) * 4 + 16)
                pe.wait_ge(sem("ex_xlo"), i + 1)
                for c in range(KC):
                    mm = pe.transpose(PS[:, 6 + k % 2, P * c:P * c + P], x_in[:, k, P * c:P * c + P], ident)
                mm.then_inc(sem("ex_xin"), 1)
            if stage(i, 3):
                j, b = i - 3, (k - 3) % 2
                pe.wait_ge(sem("ex_silu"), j + 1)
                pe.wait_ge(sem("ex_hlo"), j + 1)
                for c in range(2):
                    mm = pe.transpose(PS[:, 2 + b, P * c:P * c + P], act_h[:, b, P * c:P * c + P], ident)
                mm.then_inc(sem("ex_tr"), 1)
            if stage(i, 1):
                j, b = i - 1, (k - 1) % 2
                e = load_expert(pe, kept, j, (k - 1) % U)
                pe.wait_ge(sem("ex_xlo"), j + 3)
                pe.wait_ge(sem("ex_h"), j + 1)
                mm = pe_parts(pe, PS[:, b, :], xsT[:, b], (w13_hi, w13_lo), e)
                mm.then_inc(sem("ex_up"), 1)
            if stage(i, 4):
                j, b = i - 4, (k - 4) % 2
                e = kept_expert(pe, kept, k % U)
                pe.wait_ge(sem("ex_hlo"), j + 3)
                pe.wait_ge(sem("ex_x2"), j + 1)
                mm = pe_parts(pe, PS[:, 4 + b, 0:D], hxT[:, b], (w2_hi, w2_lo), e)
                mm.then_inc(sem("ex_down"), 1)

        pipeline(pe, 4, step)

    def act_experts(a):
        def step(i, k):
            if stage(i, 0):
                a.wait_ge(sem("ex_xin"), i + 5)
                a.wait_ge(sem("ex_up"), i + 1)
                a.copy(xsT[:, k % 2, 0], PS[:, 6 + k % 2, 0:D]).then_inc(sem("ex_xhi"), 1)
            if stage(i, 3):
                j, b = i - 3, (k - 3) % 2
                a.wait_ge(sem("ex_tr"), j + 3)
                a.wait_ge(sem("ex_down"), j + 1)
                a.copy(hxT[:, b, 0], PS[:, 2 + b, 0:HID]).then_inc(sem("ex_hhi"), 1)
            if stage(i, 2):
                j, b = i - 2, (k - 2) % U
                a.wait_ge(sem("ex_h"), j + 3)
                a.wait_ge(sem("ex_tr"), j + 1)
                a.activation(act_h[:, b % 2, 0:HID], h13[:, b, 0:HID], ACT.Silu).then_inc(sem("ex_silu"), 1)

        pipeline(a, 3, step)

    def dve_experts(v):
        kept = [v.alloc_register(f"dve_expert{k}") for k in range(U)]
        v.wait_ge(sem("expert_ids"), 1)
        v.wait_ge(sem("biases_in"), 32)
        for name in ("ex_h", "ex_x2", "ex_xlo", "ex_hlo"):
            v.sem_inc(sem(name), 2)

        def step(i, k):
            if stage(i, 0):
                v.wait_ge(sem("ex_xhi"), i + 1)
                v.tensor_tensor(xsT[:, k % 2, 1], PS[:, 6 + k % 2, 0:D], xsT[:, k % 2, 0].bitcast(F32),
                                ALU.subtract).then_inc(sem("ex_xlo"), 1)
            if stage(i, 3):
                j, b = i - 3, (k - 3) % 2
                v.wait_ge(sem("ex_hhi"), j + 1)
                v.tensor_tensor(hxT[:, b, 1], PS[:, 2 + b, 0:HID], hxT[:, b, 0].bitcast(F32),
                                ALU.subtract).then_inc(sem("ex_hlo"), 1)
            if stage(i, 1):
                j, b = i - 1, (k - 1) % U
                e = load_expert(v, kept, j, b)
                v.wait_ge(sem("ex_up"), j + 3)
                v.wait_ge(sem("ex_prod"), j + 1)
                v.tensor_tensor(h13[:, b], PS[:, b % 2, :], b13_sb[:, ds(e, 1)].rearrange("p a n -> p (a n)"),
                                ALU.add).then_inc(sem("ex_h"), 1)
            if stage(i, 4):
                j, b = i - 4, (k - 4) % U
                e = kept_expert(v, kept, b)
                v.wait_ge(sem("ex_down"), j + 3)
                v.wait_ge(sem(f"y_sent{b}"), (j - b) * 4 + 16)
                v.tensor_tensor(x2[:, b], PS[:, 4 + b % 2, 0:D], b2_sb[:, ds(e, 1)].rearrange("p a n -> p (a n)"),
                                ALU.add).then_inc(sem("ex_x2"), 1)

        pipeline(v, 4, step)

    def pool_experts(pool):
        pool.sem_inc(sem("ex_prod"), 4)
        with pool.Fori(0, SLOT_TILES // U) as it:
            for k in range(U):
                i = it * U + k
                pool.wait_ge(sem("ex_x2"), i + 3)
                pool.tensor_tensor(x2[:, k], x2[:, k], h13[:, k, HID:2 * HID], ALU.mult) \
                    .then_inc(sem("ex_prod"), 1)

    def sp_experts(sp):
        for k in range(U):
            sp.sem_inc(sem(f"y_sent{k}"), 16)
        for k in range(4):
            sp.wait_ge(sem(f"moved{k}"), LOTS)

        def load(i, k):
            sp.wait_ge(sem("ex_xin"), i + 1)
            sp.dma_start(x_in[:, k], x_slots[ds(i * P, P)]).then_inc(sem(f"x_loaded{k}"), 16)

        def store(i, k):
            sp.wait_ge(sem("ex_prod"), i + 5)
            sp.dma_start(y_slots[ds(i * P, P)], x2[:, k]).then_inc(sem(f"y_sent{k}"), 16)

        for i in range(2 * U):
            load(i, i % U)
        with sp.Fori(0, SLOT_TILES // U - 2) as it:
            for k in range(U):
                load(it * U + (2 * U + k), k)
                store(it * U + k, k)
        for i in range(SLOT_TILES - 2 * U, SLOT_TILES):
            store(i, i % U)

    with nc.allow_non_contiguous_dma(reason="minus the maxima: single values, on the general path only"), \
            nc.Block() as block:

        @block.sync
        def _(sp):
            sp_first_loads(sp)
            sp_split(sp, 0, B, plan_self)
            wait_sent(sp, J_SELF)
            A_self.sp(sp)
            redo(sp, "sp", "self", "scheck")
            sp_split(sp, J_SELF, 1, plan_k)
            sp_split(sp, J_SELF + J_K // 2, 2, plan_q)
            sp_split(sp, J_SELF + J_K // 2 + J_Q, 1, lambda it: plan_k(it + 1))
            wait_sent(sp, J_SELF + J_K + J_Q)
            sp.wait_ge(sem("vx_ps"), B * XT)
            A_cross.sp(sp, first=False)
            redo(sp, "sp", "cross", "ccheck")
            moe_loads(sp)
            sp_experts(sp)
            for t in range(TILES):
                sp.wait_ge(sem("final"), t + 1)
                sp.dma_start(out_tiles[:, t], xt[:, t]).then_inc(sem("out_sent"), 16)
            sp.wait_ge(sem("out_sent"), 16 * TILES)

        @block.gpsimd
        def _(pool):
            pool.memset(ones, 1.0).then_inc(sem("constants"), 1)
            pool.memset(eps, LN_EPS).then_inc(sem("constants"), 1)
            pool.memset(vg, 1.0).then_inc(sem("constants"), 1)
            pool.memset(normed, 0.0).then_inc(sem("constants"), 1)
            pool.memset(gate_sb, 0.0).then_inc(sem("constants"), 1)
            pool.wait_ge(sem("w_self_in"), W_SELF)
            pool.wait_ge(sem("xT"), 8)
            pool.wait_ge(sem("ln_out"), TILES)
            pool.tensor_tensor(xn, xn, bc(bo_bc.unsqueeze(1), (P, TILES, D)), ALU.add).then_inc(sem("constants"), 1)
            pool.tensor_tensor(xt, xt, bc(be_bc.unsqueeze(1), (P, TILES, D)), ALU.add).then_inc(sem("constants"), 1)
            pool.wait_ge(sem("vself_a"), 16)
            pool.wait_ge(sem("vself_b"), 16)
            A_self.pool(pool)
            pool.wait_ge(sem("constants"), 5)
            for k in range(10):
                pool.dma_start(x_slots.rearrange("(k p r) d -> k p (r d)", k=10, p=P)[k],
                               normed.rearrange("p a n -> p (a n)")).then_inc(sem("slots_zero"), 16)
            redo(pool, "pool", "self", "scheck")
            pool_cross_loads(pool)
            wait_sent(pool, J_SELF + J_K // 2 + J_Q)

            def before_k():
                pool.wait_ge(sem("vx_ps"), B * XT)
                pool.wait_ge(sem("cut_ps"), J_SELF + J_K // 2 + J_Q + 8)

            A_cross.loads(pool, 0, 0, A_cross.s("rows_free"), sem("ca_first"), before_k)
            pool.wait_ge(sem("vx_out"), B * XT)
            A_cross.pool(pool)
            redo(pool, "pool", "cross", "ccheck")
            pool_scatter(pool)
            pool_experts(pool)
            pool_gather(pool)

        @block.vector
        def _(v):
            for att in (A_self, A_cross):
                v.sem_inc(att.s("u_free"), 2)
            v.sem_inc(A_self.s("ordered"), 1)
            dve_norm(v, 0, xt, lambda v, t: v.wait_ge(sem(f"x_in{t // 4}"), 16), into(xt, xn))
            dve_split(v, 0, B, plan_self)
            move_vself(v, v.tensor_copy, sem("vself_a"), 0, (0,))
            A_self.order(v, 0, 0)
            move_vself(v, v.tensor_copy, sem("vself_a"), 0, (1,))
            A_self.dve(v)
            A_self.dve_check(v, "scheck")
            redo(v, "dve", "self", "scheck")
            dve_out_self(v)
            dve_norm(v, 2, xt, lambda v, t: v.wait_ge(sem("x1"), 2 * (t // 4) + 2),
                     lambda v, tiles: None)
            dve_split(v, J_SELF, 1, plan_k)
            dve_split(v, J_SELF + J_K // 2, 2, plan_q)
            dve_split(v, J_SELF + J_K // 2 + J_Q, 1, lambda it: plan_k(it + 1))
            v.wait_ge(sem("slots_zero"), 16 * 10)
            A_cross.dve(v)
            A_cross.dve_check(v, "ccheck")
            redo(v, "dve", "cross", "ccheck")
            dve_norm(v, 3, xt, dve_out_cross, into(xt, xn))
            dve_route(v)
            dve_shared_first(v)
            dve_experts(v)
            dve_shared_second(v)

        @block.scalar
        def _(a):
            a.wait_ge(sem("constants"), 2)
            act_norm(a, 0, 0)
            a.wait_ge(sem("w_self_in"), W_SELF)
            act_split(a, 0, B, plan_self)
            move_vself(a, a.copy, sem("vself_b"), 1)
            a.wait_ge(sem("cut_lo"), J_SELF + 2)
            A_self.act(a)
            redo(a, "act", "self", "scheck")
            act_out_self(a)
            act_values(a, 0)
            for q in range(4):
                act_std(a, 2, q)
            act_split(a, J_SELF, 1, plan_k)
            act_transpose(a, 1)
            act_split(a, J_SELF + J_K // 2, 2, plan_q)
            act_values(a, 1)
            act_split(a, J_SELF + J_K // 2 + J_Q, 1, lambda it: plan_k(it + 1))
            a.wait_ge(sem("cut_lo"), J_SELF + J_K + J_Q + 2)
            A_cross.act(a)
            redo(a, "act", "cross", "ccheck")
            act_norm(a, 3, 2)
            act_route(a)
            act_shared(a, FIRST)
            act_experts(a)
            act_shared(a, SECOND)

        @block.tensor
        def _(pe):
            for att in (A_self, A_cross):
                pe.sem_inc(att.s("rows_free"), 2)
            pe.wait_ge(sem("ident_in"), 16)
            pe_transpose(pe, 0)
            pe.wait_ge(sem("w_self_in"), W_SELF)
            pe.wait_ge(sem("xT"), 8)
            pe_split(pe, 0, B, plan_self)
            pe_vself(pe)
            pe.wait_ge(sem("vself_a"), 16)
            pe.wait_ge(sem("vself_b"), 16)
            A_self.pe(pe)
            A_self.pe_check(pe, "scheck")
            redo(pe, "pe", "self", "scheck")
            pe.wait_ge(A_self.s("step"), A_self.steps * GROUPS)
            pe_out_self(pe)
            pe.wait_ge(sem("so_y"), TILES)
            pe_values(pe, 0)
            pe_split(pe, J_SELF, 1, plan_k)
            pe.wait_ge(sem("cut_rest"), 4 + J_SELF + J_K // 2)
            pe_transpose(pe, 1)
            pe_split(pe, J_SELF + J_K // 2, 2, plan_q, before=lambda pe, it, j:
                     pe.wait_ge(sem("xT"), 13 + j))
            pe_values(pe, 1)
            pe_split(pe, J_SELF + J_K // 2 + J_Q, 1, lambda it: plan_k(it + 1))
            pe.wait_ge(sem("cut_rest"), 4 + J_SELF + J_K + J_Q)
            pe.wait_ge(sem("vx_out"), B * XT)
            pe.wait_ge(sem("ca_first"), 16 * A_cross.dmas)
            pe.sem_inc(A_cross.s("loaded0"), 16 * A_cross.dmas)
            A_cross.pe(pe)
            A_cross.pe_check(pe, "ccheck")
            redo(pe, "pe", "cross", "ccheck")
            pe.wait_ge(A_cross.s("step"), A_cross.steps * GROUPS)
            pe_out_cross(pe)
            pe.wait_ge(sem("x2"), TILES)
            pe_transpose(pe, 2)
            pe_route(pe)
            pe_shared(pe, FIRST, pe_count)
            pe_experts(pe)
            pe_shared(pe, SECOND)


def kernel(x, ctx_1024, L0_attn_wq, L0_attn_bq, L0_attn_wk, L0_attn_bk, L0_attn_wv, L0_attn_bv, L0_attn_wo,
           L0_attn_bo, L0_attn_gamma, L0_attn_beta, L0_xattn_Wq, L0_xattn_Wk, L0_xattn_Wv, L0_xattn_Wo,
           L0_ffn_gate_w, L0_ffn_w1, L0_ffn_b1, L0_ffn_w2, L0_ffn_b2, L0_ffn_w3, L0_ffn_b3, L0_ffn_sw1,
           L0_ffn_sw2, L0_ffn_sw3):
    import concourse.bacc as bacc
    from concourse.bass_utils import run_bass_kernel_spmd

    def lay(a):
        return np.ascontiguousarray(np.asarray(a))

    a = {k: np.asarray(v) for k, v in locals().items() if k[0] in "xcL"}
    arrays = {
        "x": lay(a["x"].reshape(TOK, D)),
        "ctxT": lay(a["ctx_1024"].transpose(0, 2, 1)),
        "w_self": lay(np.stack([a["L0_attn_wq"], a["L0_attn_wk"], a["L0_attn_wv"], a["L0_attn_wo"]])),
        "bqk": lay(np.stack([a["L0_attn_bq"], a["L0_attn_bk"]]).reshape(4, P).T),
        "bv": lay(a["L0_attn_bv"].reshape(1, D)),
        "bo": lay(a["L0_attn_bo"].reshape(1, D)),
        "gamma": lay(a["L0_attn_gamma"].reshape(1, D)),
        "beta": lay(a["L0_attn_beta"].reshape(1, D)),
        "w_cross": lay(np.stack([a["L0_xattn_Wq"].T, a["L0_xattn_Wk"].T, a["L0_xattn_Wv"].T])),
        "wo_cross": lay(a["L0_xattn_Wo"].T),
        "gate": lay(a["L0_ffn_gate_w"].T),
        "w13": lay(np.concatenate([a["L0_ffn_w1"].transpose(0, 2, 1), a["L0_ffn_w3"].transpose(0, 2, 1)], axis=2)),
        "b13": lay(np.concatenate([a["L0_ffn_b1"], a["L0_ffn_b3"]], axis=1)),
        "w2": lay(a["L0_ffn_w2"].transpose(0, 2, 1)),
        "b2": lay(a["L0_ffn_b2"]),
        "sw12": lay(np.concatenate([a["L0_ffn_sw1"].T, a["L0_ffn_sw2"].T], axis=1)),
        "sw3": lay(a["L0_ffn_sw3"].T),
        "ident_in": np.eye(P, dtype=np.float32),
        "lower_in": np.tril(np.ones((EXPERTS, EXPERTS), np.float32), -1),
        "before_in": np.triu(np.ones((P, P), np.float32), 1),
        "steps_in": np.arange(SLOT_TILES, dtype=np.float32).reshape(1, SLOT_TILES),
    }
    nc = bacc.Bacc("TRN2", target_bir_lowering=False, num_devices=1)
    args = [nc.dram_tensor(n, v.shape, mybir.dt.from_np(v.dtype), kind="ExternalInput").ap()
            for n, v in arrays.items()]
    args.append(nc.dram_tensor("out", (TOK, D), F32, kind="ExternalOutput").ap())
    build(nc, *args)
    r = run_bass_kernel_spmd(nc, [arrays], core_ids=[0])
    return r.results[0]["out"].reshape(B, S, D)
```
